# Optimizing a Trainium2 kernel written in Bass

```python
import numpy as np
import jax
import jax.numpy as jnp

def _softmax(x, axis=-1):
    return jax.nn.softmax(x, axis=axis)

def _gelu(x):
    return jax.nn.gelu(x, approximate=True)

def _silu(x):
    return jax.nn.silu(x)

def _sigmoid(x):
    return jax.nn.sigmoid(x)

def _layernorm(x, axis=-1, eps=1e-05):
    m = jnp.mean(x, axis=axis, keepdims=True)
    v = jnp.var(x, axis=axis, keepdims=True)
    return (x - m) / jnp.sqrt(v + eps)

def _scatter_add(tgt, idx, src, axis=0):
    return tgt.at[idx].add(src)

def _segment_sum(src, seg, n):
    return jax.ops.segment_sum(src, seg, n)
kernel_name = 'mk_adaln_ffn_d1_seqx_r2_e0f863'

def setup_inputs(seed: int=0):
    np.random.seed(seed)
    _w = jnp.asarray

    def _rec_inputs():
        import jax
        import jax.numpy as jnp
        _rk = jax.random.key(seed)
        x = -0.0003929 + 0.9999 * jax.random.normal(jax.random.fold_in(_rk, 1), (16, 512, 512), jnp.float32)
        _lenS = 512 - jax.random.randint(jax.random.fold_in(_rk, 7), (16,), 0, max(1, 512 // 4) + 1, jnp.int32)
        _lenS2 = 512 - jax.random.randint(jax.random.fold_in(_rk, 8), (16,), 0, max(1, 512 // 4) + 1, jnp.int32)
        itok_B_0_2 = jax.random.randint(jax.random.fold_in(_rk, 11), (16,), 0, 3, jnp.int32)
        return (x, itok_B_0_2)
    x, itok_B_0_2 = _rec_inputs()

    def _L0_cond_setup():
        import jax, jax.numpy as jnp
        import numpy as np
        NEG_INF = -1e+30
        key = jax.random.key(seed)
        k1, k2, k3, k4, k5 = jax.random.split(key, 5)
        B, S, D, A = (16, 512, 512, 128)
        hidden = jax.random.normal(k1, (B, S, D), dtype=jnp.float32)
        W1 = jax.random.normal(k2, (D, A), dtype=jnp.float32) / np.sqrt(D)
        b1 = jax.random.normal(k3, (A,), dtype=jnp.float32) * 0.01
        v = jax.random.normal(k4, (A,), dtype=jnp.float32) / np.sqrt(A)
        prompt_type_ids = jax.random.randint(k5, (B,), 0, 3, dtype=jnp.int32)
        return {'hidden': hidden, 'W1': W1, 'b1': b1, 'v': v, 'prompt_type_ids': prompt_type_ids}
    _L0_cond_all = _L0_cond_setup()
    _L0_cond_in = {k: v for k, v in _L0_cond_all.items() if k in ('W1', 'b1', 'v')}
    del _L0_cond_all

    def _L0_ffn_setup():
        import jax, jax.numpy as jnp
        import numpy as np
        B, S, H, F, G = (8, 1024, 512, 2048, 128)
        EPS = 1e-05

        def _dequant(q, scales, g):
            K, N = q.shape
            w = (q.astype(jnp.float32) - 128.0).reshape(K // g, g, N) * scales[:, None, :]
            return w.reshape(K, N)
        key = jax.random.key(seed)
        ks = jax.random.split(key, 8)
        x = jax.random.normal(ks[0], (B, S, H), dtype=jnp.float32)
        ln_gamma = jnp.ones((H,), jnp.float32)
        ln_beta = jnp.zeros((H,), jnp.float32)
        fc1_q = jax.random.randint(ks[1], (H, F), 0, 128, dtype=jnp.int32)
        fc2_q = jax.random.randint(ks[2], (F, H), 0, 128, dtype=jnp.int32)
        fc1_scales = jax.random.uniform(ks[3], (H // G, F), jnp.float32) * 0.02 + 0.001
        fc2_scales = jax.random.uniform(ks[4], (F // G, H), jnp.float32) * 0.02 + 0.001
        fc1_bias = jax.random.normal(ks[5], (F,), jnp.float32) * 0.02
        fc2_bias = jax.random.normal(ks[6], (H,), jnp.float32) * 0.02
        return {'x': x, 'ln_gamma': ln_gamma, 'ln_beta': ln_beta, 'fc1_q': fc1_q, 'fc1_scales': fc1_scales, 'fc1_bias': fc1_bias, 'fc2_q': fc2_q, 'fc2_scales': fc2_scales, 'fc2_bias': fc2_bias}
    _L0_ffn_all = _L0_ffn_setup()
    _L0_ffn_in = {k: v for k, v in _L0_ffn_all.items() if k in ('ln_gamma', 'ln_beta', 'fc1_q', 'fc1_scales', 'fc1_bias', 'fc2_q', 'fc2_scales', 'fc2_bias')}
    del _L0_ffn_all
    return {'x': x, 'itok_B_0_2': itok_B_0_2, 'L0_cond_W1': _L0_cond_in['W1'], 'L0_cond_b1': _L0_cond_in['b1'], 'L0_cond_v': _L0_cond_in['v'], 'L0_ffn_ln_gamma': _L0_ffn_in['ln_gamma'], 'L0_ffn_ln_beta': _L0_ffn_in['ln_beta'], 'L0_ffn_fc1_q': _L0_ffn_in['fc1_q'], 'L0_ffn_fc1_scales': _L0_ffn_in['fc1_scales'], 'L0_ffn_fc1_bias': _L0_ffn_in['fc1_bias'], 'L0_ffn_fc2_q': _L0_ffn_in['fc2_q'], 'L0_ffn_fc2_scales': _L0_ffn_in['fc2_scales'], 'L0_ffn_fc2_bias': _L0_ffn_in['fc2_bias']}

def reference(x, itok_B_0_2, L0_cond_W1, L0_cond_b1, L0_cond_v, L0_ffn_ln_gamma, L0_ffn_ln_beta, L0_ffn_fc1_q, L0_ffn_fc1_scales, L0_ffn_fc1_bias, L0_ffn_fc2_q, L0_ffn_fc2_scales, L0_ffn_fc2_bias):
    import jax
    import jax.numpy as jnp

    def _L0_cond_ref(hidden, W1, b1, v, prompt_type_ids):
        import jax, jax.numpy as jnp
        import numpy as np
        NEG_INF = -1e+30
        B, S, D = hidden.shape
        attn_in = jnp.tanh(jnp.einsum('bsd,da->bsa', hidden, W1) + b1)
        scores = jnp.einsum('bsa,a->bs', attn_in, v)
        idx = jnp.arange(S)
        j = idx[:, None]
        l = idx[None, :]
        prefix_m = l <= j
        postfix_m = l >= j
        cloze_m = l != j
        pt = prompt_type_ids[:, None, None]
        mask = jnp.where(pt == 0, prefix_m[None], jnp.where(pt == 1, postfix_m[None], cloze_m[None]))
        masked_scores = jnp.where(mask, scores[:, None, :], NEG_INF)
        p = jax.nn.softmax(masked_scores, axis=-1)
        cnt = jnp.sum(mask, axis=-1).astype(hidden.dtype)
        pooled = jnp.einsum('bjl,bld->bjd', p, hidden) / cnt[..., None]
        return pooled

    def _L0_ffn_ref(x, ln_gamma, ln_beta, fc1_q, fc1_scales, fc1_bias, fc2_q, fc2_scales, fc2_bias):
        import jax, jax.numpy as jnp
        import numpy as np
        B, S, H, F, G = (8, 1024, 512, 2048, 128)
        EPS = 1e-05

        def _dequant(q, scales, g):
            K, N = q.shape
            w = (q.astype(jnp.float32) - 128.0).reshape(K // g, g, N) * scales[:, None, :]
            return w.reshape(K, N)
        residual = x
        mu = jnp.mean(x, axis=-1, keepdims=True)
        var = jnp.mean(jnp.square(x - mu), axis=-1, keepdims=True)
        h = (x - mu) * jax.lax.rsqrt(var + EPS) * ln_gamma + ln_beta
        hf = h.reshape(-1, H)
        w1 = _dequant(fc1_q, fc1_scales, G)
        y = hf @ w1 + fc1_bias
        y = jax.nn.silu(y)
        w2 = _dequant(fc2_q, fc2_scales, G)
        z = y @ w2 + fc2_bias
        return residual + 0.5 * z.reshape(residual.shape)
    x = x + _L0_ffn_ref(_L0_cond_ref(x, L0_cond_W1, L0_cond_b1, L0_cond_v, itok_B_0_2), L0_ffn_ln_gamma, L0_ffn_ln_beta, L0_ffn_fc1_q, L0_ffn_fc1_scales, L0_ffn_fc1_bias, L0_ffn_fc2_q, L0_ffn_fc2_scales, L0_ffn_fc2_bias)
    return x

_drawn_inputs = setup_inputs


def setup_inputs(seed=0):
    import zlib

    import numpy as np

    out = dict(_drawn_inputs(seed))
    spreads = {'L0_ffn_ln_gamma': (1.0, 0.2), 'L0_ffn_ln_beta': (0.0, 0.1)}
    factors = {'L0_cond_b1': 64.0, 'L0_ffn_fc1_bias': 64.0, 'L0_ffn_fc2_bias': 64.0}
    for name, (base, spread) in spreads.items():
        noise = np.random.default_rng([zlib.crc32(name.encode()), seed]).standard_normal(out[name].shape)
        drawn = base * np.exp(spread * noise) if base else spread * noise
        out[name] = jnp.asarray(drawn.astype(out[name].dtype))
    for name, factor in factors.items():
        out[name] = (out[name] * factor).astype(out[name].dtype)
    return out
```

```python
from contextlib import ExitStack

import concourse.bass as bass
from concourse import mybir

ALU = mybir.AluOpType
ACT = mybir.ActivationFunctionType
AX_X = mybir.AxisListType.X
F32 = mybir.dt.float32
F32R = mybir.dt.float32r
I32 = mybir.dt.int32

P = 128
NEG = -1e30
EPS = 1e-5


def build(nc, x, itok, cond_w, cond_b, cond_v, gamma, beta, fc1_q, fc1_s, fc1_b, fc2_q, fc2_s, fc2_b, out):
    B, S, D = x.shape
    F = fc1_q.shape[1]
    NJ = S // P
    ND = D // P
    NF = F // P
    UNIT = 512
    NQ = F // UNIT
    assert cond_w.shape == [D, P] or tuple(cond_w.shape) == (D, P)
    assert S == 512 and D == 512 and NJ == 4 and ND == 4 and NF == 16 and B % 2 == 0
    NPREP = ND * NQ + NF
    SLOT = 514
    POOL_CONSTS = 26
    A_STEPS = 47

    with ExitStack() as ctx:
        def sb(name, shape, dt=F32):
            return ctx.enter_context(nc.sbuf_tensor(name, shape, dt))

        def sem(name):
            return ctx.enter_context(nc.semaphore(name))

        w1_hi = sb("w1_hi", [P, ND, F], F32R)
        w1_lo = sb("w1_lo", [P, ND, F], F32R)
        w2_hi = sb("w2_hi", [P, NF, D], F32R)
        w2_lo = sb("w2_lo", [P, NF, D], F32R)
        wc_hi = sb("wc_hi", [P, ND, P], F32R)
        wc_lo = sb("wc_lo", [P, ND, P], F32R)
        hT_hi = sb("hT_hi", [P, ND, S], F32R)
        hT_lo = sb("hT_lo", [P, ND, S], F32R)
        xt = [sb(f"x{p}", [P, NJ, D]) for p in range(2)]
        scratch = sb("scratch", [P, NJ * SLOT])
        xs_hi = sb("xs_hi", [P, D], F32R)
        xs_lo = sb("xs_lo", [P, D], F32R)
        part_hi = sb("part_hi", [P, S], F32R)
        part_lo = sb("part_lo", [P, S], F32R)
        coef_hi = sb("coef_hi", [P, S], F32R)
        coef_lo = sb("coef_lo", [P, S], F32R)
        e_cols = sb("e_cols", [P, NJ, P], F32R)
        u_rows = sb("u_rows", [P, D], F32R)
        u_sums = sb("u_sums", [P, 2], F32R)
        y_f = [sb(f"y_f{i}", [P, S]) for i in range(2)]
        y_hi = [sb(f"y_hi{i}", [P, S], F32R) for i in range(2)]
        y_lo = [sb(f"y_lo{i}", [P, S], F32R) for i in range(2)]
        b2h = sb("b2h", [P, D])
        stage_s = [y_f[0], y_f[1], b2h, sb("stage_s3", [P, UNIT])]
        ident = sb("ident", [P, P])
        v_bc = sb("v_bc", [P, P])
        sgn = sb("sgn", [P, P])
        sgn_blk = sb("sgn_blk", [P, NJ])
        pen_sel = sb("pen_sel", [P, NJ])
        pen_own = sb("pen_own", [P, NJ])
        ones2 = sb("ones2", [P, 2], F32R)
        b1c = sb("b1c", [P, 1])
        v_col = sb("v_col", [P, 1])
        gam = sb("gam", [P, ND])
        bet = sb("bet", [P, ND])
        b1 = sb("b1", [P, NF])
        b1x = sb("b1x", [P, NF])
        tok_i = sb("tok_i", [P, B], I32)
        tok = sb("tok", [P, B])
        is0 = sb("is0", [P, B])
        is1 = sb("is1", [P, B])
        row_i = sb("row_i", [P, NJ], I32)
        row_f = sb("row_f", [P, NJ])
        row_a = sb("row_a", [P, NJ])
        row_b = sb("row_b", [P, NJ])
        par = sb("par", [P, B, 8])
        cur = sb("cur", [P, 8])
        pen_p = sb("pen_p", [P, P])
        columns4 = sb("columns4", [P, 14 * NJ])
        taken = iter(range(14))

        def small():
            k = next(taken)
            return columns4[:, k * NJ:(k + 1) * NJ]

        pen_c = small()
        blk_max = small()
        s_col = small()
        e_arg = small()
        e_f = small()
        m_sel = small()
        m_col = sb("m_col", [P, 1])
        dcnt = small()
        c_row = small()
        stats = sb("stats", [P, NJ, 6])
        mv = sb("mv", [P, NJ, 2])
        ve = small()
        nt = small()
        rs_i = small()
        one_col = small()
        rstd = [small() for _ in range(2)]

        th = scratch[:, 0:S]
        sc_row = scratch[:, SLOT:SLOT + S]
        fwd = scratch[:, 2 * SLOT:2 * SLOT + S + 1]
        bwd = scratch[:, 3 * SLOT:3 * SLOT + S + 1]
        p_f = scratch[:, 2 * SLOT:2 * SLOT + S]
        c_f = scratch[:, 3 * SLOT:3 * SLOT + S]
        pooled = [scratch[:, J * SLOT:J * SLOT + D] for J in range(NJ)]
        wc_f = scratch[:, SLOT:SLOT + ND * P]

        def by_block(ap):
            return ap.rearrange("p (j n) -> p j n", j=NJ)

        def f32(ap):
            return ap.bitcast(F32)

        def bank(name):
            return ctx.enter_context(nc.psum_tensor(name, [P, 512], F32))

        z_ps = [bank(f"z_ps{r}") for r in range(NJ)]
        y_ps = [bank(f"y_ps{i}") for i in range(2)]
        a_ps = [bank(f"a_ps{i}") for i in range(2)]

        const_in = sem("const_in")
        bias_in = sem("bias_in")
        x_in = [sem(f"x_in{J}") for J in range(NJ)]
        stored = [sem(f"stored{J}") for J in range(NJ)]
        pool_const = sem("pool_const")
        pool_step = sem("pool_step")
        dve_const = sem("dve_const")
        dve_step = sem("dve_step")
        consts_ready = sem("consts_ready")
        q_in = [sem(f"q_in{j}") for j in range(4)]
        s_in = [sem(f"s_in{j}") for j in range(4)]
        wf_ready = sem("wf_ready")
        wg_ready = sem("wg_ready")
        whi_ready = sem("whi_ready")
        w_ready = sem("w_ready")
        beta_done = sem("beta_done")
        b1_ready = sem("b1_ready")
        xt_tr = sem("xt_tr")
        xt_hi = sem("xt_hi")
        xt_ready = sem("xt_ready")
        at_done = sem("at_done")
        tanh_done = sem("tanh_done")
        sc_mm = sem("sc_mm")
        sc_ready = sem("sc_ready")
        args_ready = sem("args_ready")
        exp_done = sem("exp_done")
        e_ready = sem("e_ready")
        pc_ready = sem("pc_ready")
        xs_ready = sem("xs_ready")
        xs_used = sem("xs_used")
        usum_done = sem("usum_done")
        usum_ready = sem("usum_ready")
        dsum_done = sem("dsum_done")
        c_ready = sem("c_ready")
        u_hi = sem("u_hi")
        u_ready = sem("u_ready")
        pz_done = sem("pz_done")
        pooled_done = sem("pooled_done")
        res_added = sem("res_added")
        bias_added = sem("bias_added")
        h_ready = sem("h_ready")
        h_tr = sem("h_tr")
        hT_hi_done = sem("hT_hi_done")
        hT_done = sem("hT_done")
        fc1_done = sem("fc1_done")
        silu_done = sem("silu_done")
        yhi_done = sem("yhi_done")
        split_done = sem("split_done")
        fc2_done = sem("fc2_done")
        final_done = sem("final_done")

        LAST = 2 * NF - 4
        PE_PLAN = {3: [("T", 0)], 4: [("AT", 0), ("T", 1)], 5: [("AT", 1), ("T", 2)], 6: [("AT", 2), ("T", 3)],
                   7: [("AT", 3)], 8: [("SC", 0)], 13: [("U", 0)], 14: [("U", 1), ("USUM", 0)], 15: [("U", 2)],
                   16: [("U", 3), ("DSUM", 0)], 17: [("PZ", 0)], 18: [("PZ", 1)], 19: [("PZ", 2)], 20: [("PZ", 3)]}
        ACT_PLAN = {3: [("XT", 0)], 4: [("XT", 1)], 5: [("XT", 2)], 6: [("XT", 3)], 7: [("TANH", 0)],
                    8: [("SC", 0)], 12: [("EXP", 0)], 16: [("U", 0)], 17: [("PZ", 0)], 18: [("PZ", 1)],
                    19: [("PZ", 2)], 20: [("PZ", 3)]}
        DVE_PLAN = {3: [("XT", 0)], 4: [("XT", 1)], 5: [("XT", 2)], 6: [("XT", 3)], 7: [("PAR", 0)],
                    8: [("SCAN", 0)], 9: [("COLS", 0)], 10: [("ROWMAX", 0)], 11: [("ARGS", 0)], 12: [("E", 0)],
                    13: [("PC", 0)], 14: [("USUM", 0)], 16: [("DSUM", 0), ("U", 0)], 17: [("LN", 0)],
                    18: [("LN", 1)], 19: [("LN", 2)], 20: [("LN", 3)], 21: [("RSTD", 0)], 22: [("H", 0)]}

        def in_order(plan):
            return [step for h in sorted(plan) for step in plan[h]]

        stage_q = [xt[1][:, j, :] for j in range(4)]

        block = ctx.enter_context(nc.Block())

        @block.sync
        def _(sp):
            x_dram = x.rearrange("b (j p) d -> (b j) p d", p=P)
            out_dram = out.rearrange("b (j p) d -> (b j) p d", p=P)

            def load_x(a, p):
                for J in range(NJ):
                    sp.dma_start(xt[p][:, J, :], x_dram[bass.ds(a * NJ + J, 1), :, :].rearrange("a p d -> p (a d)")).then_inc(x_in[J], 16)

            def store(b, p, J):
                sp.wait_ge(final_done, b * NJ + (J + 1))
                sp.dma_start(out_dram[bass.ds(b * NJ + J, 1), :, :].rearrange("a p d -> p (a d)"), xt[p][:, J, :]).then_inc(stored[J], 16)

            load_x(0, 0)
            sp.dma_start(wc_f.rearrange("p (c a) -> p c a", c=ND), cond_w.rearrange("(c p) a -> p c a", p=P)).then_inc(const_in, 16)
            sp.dma_start(b1c[:], cond_b.rearrange("(p o) -> p o", o=1)).then_inc(const_in, 16)
            sp.dma_start(v_col[:], cond_v.rearrange("(p o) -> p o", o=1)).then_inc(const_in, 16)
            sp.dma_start(gam[:], gamma.rearrange("(c p) -> p c", p=P), allow_slow_non_contiguous=True).then_inc(const_in, 16)
            sp.dma_start(bet[:], beta.rearrange("(c p) -> p c", p=P), allow_slow_non_contiguous=True).then_inc(const_in, 16)
            sp.dma_start(b1x[:], fc1_b.rearrange("(c p) -> p c", p=P), allow_slow_non_contiguous=True).then_inc(const_in, 16)
            sp.dma_start(tok_i[:], itok.rearrange("(o d) -> o d", o=1).to_broadcast([P, B])).then_inc(const_in, 16)

            def load_unit(i, j, q_src, s_src, wait):
                if wait is not None:
                    sp.wait_ge(w_ready, i * 4 + (j - 3))
                    sp.wait_ge(beta_done, wait)
                sp.dma_start(stage_q[j].bitcast(I32), q_src).then_inc(q_in[j], 16)
                sp.dma_start(stage_s[j][:], s_src.to_broadcast([P, UNIT])).then_inc(s_in[j], 16)

            def load_w1(i, wait):
                for j in range(NQ):
                    load_unit(i, j, fc1_q[bass.ds(i * P, P), j * UNIT:(j + 1) * UNIT],
                              fc1_s[bass.ds(i, 1), j * UNIT:(j + 1) * UNIT], i * 4 + (j - 3) if wait else None)

            def load_w2(i):
                for j in range(4):
                    load_unit(i + ND, j, fc2_q[bass.ds((i * 4 + j) * P, P), :],
                              fc2_s[bass.ds(i * 4 + j, 1), :], ND * NQ)

            load_w1(0, False)
            with sp.Fori(1, ND) as i:
                load_w1(i, True)
            with sp.Fori(0, NF // 4) as i:
                load_w2(i)
            sp.wait_ge(w_ready, NPREP)
            sp.dma_start(b2h[:], fc2_b.rearrange("(o d) -> o d", o=1).to_broadcast([P, D])).then_inc(bias_in, 16)
            load_x(1, 1)

            def turn(b, p):
                for J in range(NJ):
                    store(b - 1, p, J)
                for J in range(NJ):
                    sp.wait_ge(stored[J], b * 16)
                    sp.dma_start(xt[p][:, J, :], x_dram[bass.ds((b + 1) * NJ + J, 1), :, :].rearrange("a p d -> p (a d)")).then_inc(x_in[J], 16)

            with sp.Fori(0, B // 2 - 1) as i:
                turn(i * 2 + 1, 0)
                turn(i * 2 + 2, 1)
            for b in (B - 2, B - 1):
                for J in range(NJ):
                    store(b, b % 2, J)
            for J in range(NJ):
                sp.wait_ge(stored[J], 16 * B)

        @block.gpsimd
        def _(pool):
            done = [0]

            def link(ins):
                done[0] += 1
                ins.then_inc(pool_const, 1)
                pool.wait_ge(pool_const, done[0])

            link(nc.gpsimd.memset(ident[:], 0.0))
            link(nc.gpsimd.affine_select(out=ident[:], in_=ident[:], compare_op=ALU.not_equal, fill=1.0, base=0,
                                         pattern=[[-1, P]], channel_multiplier=1))
            link(nc.gpsimd.memset(sgn[:], 0.0))
            link(nc.gpsimd.affine_select(out=sgn[:], in_=sgn[:], compare_op=ALU.is_ge, fill=1.0, base=0,
                                         pattern=[[-1, P]], channel_multiplier=1))
            link(nc.gpsimd.affine_select(out=sgn[:], in_=sgn[:], compare_op=ALU.is_ge, fill=-1.0, base=0,
                                         pattern=[[1, P]], channel_multiplier=-1))
            link(nc.gpsimd.memset(sgn_blk[:], 0.0))
            link(nc.gpsimd.memset(pen_sel[:], 0.0))
            link(nc.gpsimd.memset(pen_own[:], 0.0))
            for q in range(4):
                rows = slice(32 * q, 32 * q + 32)
                link(nc.gpsimd.affine_select(out=sgn_blk[rows, :], in_=sgn_blk[rows, :], compare_op=ALU.is_ge,
                                             fill=1.0, base=0, pattern=[[-1, NJ]], channel_multiplier=1))
                link(nc.gpsimd.affine_select(out=sgn_blk[rows, :], in_=sgn_blk[rows, :], compare_op=ALU.is_ge,
                                             fill=-1.0, base=0, pattern=[[1, NJ]], channel_multiplier=-1))
                link(nc.gpsimd.affine_select(out=pen_sel[rows, :], in_=pen_sel[rows, :], compare_op=ALU.is_equal,
                                             fill=NEG, base=0, pattern=[[1, NJ]], channel_multiplier=-1))
                link(nc.gpsimd.affine_select(out=pen_own[rows, :], in_=pen_own[rows, :], compare_op=ALU.not_equal,
                                             fill=NEG, base=0, pattern=[[1, NJ]], channel_multiplier=-1))
            link(nc.gpsimd.iota(row_i[:], pattern=[[P, NJ]], base=0, channel_multiplier=1))

            link(nc.gpsimd.memset(one_col, 1.0))
            assert done[0] == POOL_CONSTS

            def split_x(a, p, n):
                J = n % NJ
                if n < NJ:
                    pool.wait_ge(x_in[J], a * 16 + 16)
                pool.wait_ge(xs_used, a * 8 + n)
                nc.gpsimd.tensor_tensor(xs_hi[:], xt[p][:, J, :], one_col[:, 0:1].to_broadcast([P, D]),
                                        ALU.mult).then_inc(pool_step, 1)
                pool.wait_ge(pool_step, a * 8 + (n + 1))
                nc.gpsimd.tensor_tensor(xs_lo[:], xt[p][:, J, :], f32(xs_hi[:]), ALU.subtract).then_inc(xs_ready, 1)

            def add_bias(a, p, J):
                pool.wait_ge(res_added, a * NJ + (J + 1))
                nc.gpsimd.tensor_tensor(xt[p][:, J, :], xt[p][:, J, :], b2h[:], ALU.add).then_inc(bias_added, 1)

            def stage_a(a, p, first=False):
                for n in range(8):
                    split_x(a, p, n)
                if first:
                    pool.wait_ge(bias_in, 16)
                    link(nc.gpsimd.tensor_scalar(b2h[:], b2h[:], 0.5, None, ALU.mult))
                for J in range(NJ):
                    add_bias(a, p, J)

            stage_a(0, 0, True)
            with pool.Fori(0, B // 2 - 1) as i:
                stage_a(i * 2 + 1, 1)
                stage_a(i * 2 + 2, 0)
            stage_a(B - 1, 1)

        @block.scalar
        def _(act):
            def copy(o, i):
                return nc.scalar.activation(o, i, ACT.Copy)

            def xt_hi_part(a, s):
                act.wait_ge(xt_tr, a * NJ + (s + 1))
                if s:
                    act.wait_ge(at_done, a * NJ + s)
                copy(part_hi[:], a_ps[0][:]).then_inc(xt_hi, 1)

            def tanh(a, _):
                act.wait_ge(at_done, a * NJ + NJ)
                nc.scalar.activation(th, a_ps[1][:], ACT.Tanh, bias=b1c[:, 0:1]).then_inc(tanh_done, 1)

            def scores(a, _):
                act.wait_ge(sc_mm, a + 1)
                copy(sc_row, a_ps[0][:]).then_inc(sc_ready, 1)

            def exps(a, _):
                act.wait_ge(args_ready, a + 1)
                nc.scalar.activation(e_f[:], e_arg[:], ACT.Exp).then_inc(exp_done, 1)
                nc.scalar.activation(c_f, c_f, ACT.Exp, bias=m_col[:, 0:1]).then_inc(exp_done, 1)
                for J in range(NJ):
                    blk = p_f[:, J * P:(J + 1) * P]
                    nc.scalar.activation(blk, blk, ACT.Exp, bias=s_col[:, J:J + 1]).then_inc(exp_done, 1)

            def u_hi_part(a, _):
                act.wait_ge(xs_used, a * 8 + NJ)
                copy(u_rows[:], a_ps[0][:]).then_inc(u_hi, 1)

            def pool_rows(a, J):
                if J == 0:
                    act.wait_ge(c_ready, a + 1)
                act.wait_ge(pz_done, a * NJ + (J + 1))
                nc.scalar.activation(pooled[J], a_ps[J % 2][:], ACT.Copy, scale=c_row[:, J:J + 1]).then_inc(pooled_done, 1)

            def h_hi_part(a, c):
                if c == 0 and not (isinstance(a, int) and a == 0):
                    act.wait_ge(fc1_done, a * NF)
                act.wait_ge(h_tr, a * ND + (c + 1))
                copy(hT_hi[:, c, :], a_ps[c % 2][:]).then_inc(hT_hi_done, 1)

            steps = {"XT": xt_hi_part, "TANH": tanh, "SC": scores, "EXP": exps, "U": u_hi_part, "PZ": pool_rows}

            def silu(b, k):
                act.wait_ge(fc1_done, b * NF + (k + 1))
                if k >= 2 or not (isinstance(b, int) and b == 0):
                    act.wait_ge(split_done, b * NF + (k - 1))
                nc.scalar.activation(y_f[k % 2][:], y_ps[k % 2][:], ACT.Silu, bias=b1[:, k:k + 1]).then_inc(silu_done, 1)

            def ffn(b, with_a, first=False):
                for k in range(2):
                    if first:
                        silu(b, k)
                    else:
                        act.wait_ge(fc1_done, b * NF + (k + 1))
                        act.wait_ge(split_done, b * NF + (k - 1))
                        nc.scalar.activation(y_f[k % 2][:], y_ps[k % 2][:], ACT.Silu,
                                             bias=b1[:, k:k + 1]).then_inc(silu_done, 1)
                for h in range(LAST):
                    if h % 2 == 0:
                        silu(b, h // 2 + 2)
                    if with_a:
                        for name, n in ACT_PLAN.get(h, []):
                            steps[name](b + 1, n)
                if with_a:
                    for c in range(ND):
                        h_hi_part(b + 1, c)

            def split_w(i, j, dst):
                act.wait_ge(wg_ready, i * 4 + (j + 1))
                copy(dst, stage_s[j][:]).then_inc(whi_ready, 1)

            w1_flat = w1_hi[:].rearrange("p c f -> p (c f)")
            w2_flat = w2_hi[:].rearrange("p c f -> p (c f)")
            act.wait_ge(consts_ready, 1)
            for name, n in in_order(ACT_PLAN):
                steps[name](0, n)
            for c in range(ND):
                h_hi_part(0, c)
            with act.Fori(0, ND) as i:
                for j in range(NQ):
                    split_w(i, j, w1_flat[:, bass.ds(i * F + j * UNIT, UNIT)])
            with act.Fori(0, NF // 4) as i:
                for j in range(4):
                    split_w(i + ND, j, w2_flat[:, bass.ds((i * 4 + j) * D, D)])
            act.wait_ge(b1_ready, 1)
            ffn(0, True, True)
            ffn(1, True)
            with act.Fori(1, B // 2 - 1) as i:
                ffn(i * 2, True)
                ffn(i * 2 + 1, True)
            ffn(B - 2, True)
            ffn(B - 1, False)

        @block.vector
        def _(dve):
            v = nc.vector
            done = [0]

            def link(ins):
                done[0] += 1
                ins.then_inc(dve_const, 1)
                dve.wait_ge(dve_const, done[0])

            link(v.memset(f32(e_cols[:]), 0.0))
            link(v.memset(f32(ones2[:]), 1.0))
            dve.wait_ge(const_in, 16 * 7)
            link(v.tensor_copy(v_bc[:], v_col[:, 0:1].to_broadcast([P, P])))
            wc_flat = [t[:].rearrange("p c a -> p (c a)") for t in (wc_hi, wc_lo)]
            link(v.tensor_copy(wc_flat[0], wc_f))
            link(v.tensor_tensor(wc_flat[1], wc_f, f32(wc_flat[0]), ALU.subtract))
            link(v.tensor_copy(tok[:], tok_i[:]))
            link(v.tensor_scalar(is0[:], tok[:], 0.0, None, ALU.is_equal))
            link(v.tensor_scalar(is1[:], tok[:], 1.0, None, ALU.is_equal))
            link(v.tensor_tensor(par[:, :, 0], is1[:], is0[:], ALU.subtract))
            link(v.tensor_scalar(par[:, :, 1], tok[:], 0.0, NEG, ALU.not_equal, ALU.mult))
            link(v.tensor_scalar(par[:, :, 2], tok[:], 1.0, NEG, ALU.not_equal, ALU.mult))
            link(v.tensor_scalar(par[:, :, 3], par[:, :, 0], 0.0, NEG, ALU.not_equal, ALU.mult))
            dve.wait_ge(pool_const, POOL_CONSTS)
            link(v.tensor_copy(row_f[:], row_i[:]))
            link(v.tensor_scalar(row_a[:], row_f[:], float(S - 2), None, ALU.subtract))
            link(v.tensor_scalar(row_b[:], row_f[:], -1.0, 1.0, ALU.mult, ALU.add))
            for J in range(NJ):
                cnt = par[:, :, 4 + J]
                link(v.tensor_scalar(cnt, is0[:], row_a[:, J:J + 1], float(S - 1), ALU.mult, ALU.add))
                link(v.scalar_tensor_tensor(cnt, is1[:], row_b[:, J:J + 1], cnt, ALU.mult, ALU.add))
            v.tensor_copy(b1[:], b1x[:]).then_inc(consts_ready, 1)

            class Chain:
                def __init__(self, a):
                    self.base, self.n = a * A_STEPS, 0

                def __call__(self, ins):
                    self.n += 1
                    ins.then_inc(dve_step, 1)
                    dve.wait_ge(dve_step, self.base + self.n)

            def xt_lo_part(a, s, p, ch):
                dve.wait_ge(xt_hi, a * NJ + (s + 1))
                v.tensor_tensor(part_lo[:], a_ps[0][:], f32(part_hi[:]), ALU.subtract).then_inc(xt_ready, 1)

            def params(a, _, p, ch):
                flat = par[:].rearrange("p b k -> p (b k)")
                ch(v.tensor_copy(cur[:], flat[:, bass.ds(a * 8, 8)]))
                ch(v.tensor_scalar(pen_p[:], sgn[:], cur[:, 0:1], NEG, ALU.is_equal, ALU.mult))
                ch(v.tensor_scalar(pen_c[:], sgn_blk[:], cur[:, 0:1], NEG, ALU.is_equal, ALU.mult))
                ch(v.tensor_tensor(pen_c[:], pen_c[:], pen_own[:], ALU.min))

            def scans(a, _, p, ch):
                dve.wait_ge(sc_ready, a + 1)
                ch(v.memset(fwd[:, 0:1], NEG))
                ch(v.memset(bwd[:, S:S + 1], NEG))
                ch(v.tensor_tensor_scan(fwd[:, 1:S + 1], sc_row, sc_row, NEG, ALU.max, ALU.max))
                ch(v.tensor_tensor_scan(bwd[:, 0:S][:, ::-1], sc_row[:, ::-1], sc_row[:, ::-1], NEG, ALU.max, ALU.max))

            def columns(a, _, p, ch):
                ch(v.tensor_reduce(blk_max[:], by_block(sc_row), AX_X, ALU.max))
                ch(v.tensor_tensor(by_block(th), by_block(sc_row), ident[:].rearrange("p (o n) -> p o n", o=1).to_broadcast([P, NJ, P]), ALU.mult))
                ch(v.tensor_reduce(s_col[:], by_block(th), AX_X, ALU.add))
                ch(v.tensor_tensor(e_arg[:], s_col[:], blk_max[:], ALU.subtract))
                ch(v.tensor_tensor(m_sel[:], blk_max[:], pen_sel[:], ALU.add))
                ch(v.tensor_reduce(m_col[:], m_sel[:], AX_X, ALU.max))

            def row_max(a, _, p, ch):
                ch(v.tensor_tensor(th, fwd[:, 0:S], bwd[:, 1:S + 1], ALU.max))
                ch(v.tensor_scalar(sc_row, fwd[:, 1:S + 1], cur[:, 1:2], None, ALU.add))
                ch(v.scalar_tensor_tensor(sc_row, bwd[:, 0:S], cur[:, 2:3], sc_row, ALU.add, ALU.max))
                ch(v.scalar_tensor_tensor(sc_row, th, cur[:, 3:4], sc_row, ALU.add, ALU.max))

            def exp_args(a, _, p, ch):
                ch(v.tensor_tensor(by_block(p_f), pen_p[:].rearrange("p (o n) -> p o n", o=1).to_broadcast([P, NJ, P]), by_block(sc_row), ALU.subtract))
                v.tensor_tensor(by_block(c_f), pen_c[:].rearrange("p (n o) -> p n o", o=1).to_broadcast([P, NJ, P]), by_block(sc_row),
                                ALU.subtract).then_inc(args_ready, 1)

            def split_e(a, _, p, ch):
                dve.wait_ge(exp_done, a * 6 + 1)
                flat = e_cols[:].rearrange("p l m -> p (l m)")

                def diag(q):
                    return flat[:, 32 * q:32 * q + (NJ - 1) * (P + 1) + 1:P + 1]
                ch(v.tensor_copy(diag(0), e_f[:]))
                ch(v.tensor_copy(diag(2), e_f[:]))
                ch(v.tensor_tensor(diag(1), e_f[:], f32(diag(0)), ALU.subtract))
                v.tensor_tensor(diag(3), e_f[:], f32(diag(0)), ALU.subtract).then_inc(e_ready, 1)

            def split_pc(a, _, p, ch):
                dve.wait_ge(exp_done, a * 6 + 6)
                ch(v.tensor_copy(part_hi[:], p_f))
                ch(v.tensor_tensor(part_lo[:], p_f, f32(part_hi[:]), ALU.subtract))
                ch(v.tensor_copy(coef_hi[:], c_f))
                v.tensor_tensor(coef_lo[:], c_f, f32(coef_hi[:]), ALU.subtract).then_inc(pc_ready, 1)

            def split_usum(a, _, p, ch):
                dve.wait_ge(usum_done, a + 1)
                ch(v.tensor_copy(u_sums[:], a_ps[1][:, 0:2]))
                v.tensor_tensor(u_sums[64:, :], a_ps[1][64:, 0:2], f32(u_sums[64:, :]), ALU.subtract).then_inc(usum_ready, 1)

            def row_scale(a, _, p, ch):
                dve.wait_ge(dsum_done, a + 1)
                ch(v.tensor_tensor(dcnt[:], a_ps[1][:, 2:2 + 2 * NJ:2], cur[:, 4:4 + NJ], ALU.mult))
                v.reciprocal(c_row[:], dcnt[:]).then_inc(c_ready, 1)

            def split_u(a, _, p, ch):
                dve.wait_ge(u_hi, a + 1)
                v.tensor_tensor(u_rows[64:, :], a_ps[0][64:, :], f32(u_rows[64:, :]), ALU.subtract).then_inc(u_ready, 1)

            def row_stats(a, J, p, ch):
                dve.wait_ge(pooled_done, a * NJ + (J + 1))
                ch(v.bn_stats(stats[:, J, :], pooled[J]))
                dve.wait_ge(xs_ready, a * 8 + (NJ + J + 1))
                v.tensor_tensor(xt[p][:, J, :], xt[p][:, J, :], pooled[J], ALU.add).then_inc(res_added, 1)
                ch(v.bn_aggr(mv[:, J, :], stats[:, J, :]))

            def row_rstd(a, _, p, ch):
                ch(v.tensor_scalar(ve[:], mv[:, :, 1], EPS, None, ALU.add))
                ch(v.tensor_scalar(rs_i[:].bitcast(I32), ve[:].bitcast(I32), 1, None, ALU.logical_shift_right))
                ch(v.tensor_scalar(rstd[0][:].bitcast(I32), rs_i[:].bitcast(I32), -1.0, float(0x5f3759df), ALU.mult, ALU.add))
                for n in range(3):
                    y, new = rstd[n % 2], rstd[(n + 1) % 2]
                    ch(v.tensor_tensor(nt[:], y[:], y[:], ALU.mult))
                    ch(v.scalar_tensor_tensor(nt[:], nt[:], -0.5, ve[:], ALU.mult, ALU.mult))
                    ch(v.scalar_tensor_tensor(new[:], nt[:], 1.5, y[:], ALU.add, ALU.mult))

            def normalise(a, _, p, ch):
                dve.wait_ge(res_added, a * NJ + NJ)
                for J in range(NJ):
                    v.tensor_scalar(pooled[J], pooled[J], mv[:, J, 0:1], rstd[1][:, J:J + 1], ALU.subtract,
                                    ALU.mult).then_inc(h_ready, 1)

            def h_lo_part(a, c):
                dve.wait_ge(hT_hi_done, a * ND + (c + 1))
                v.tensor_tensor(hT_lo[:, c, :], a_ps[c % 2][:], f32(hT_hi[:, c, :]), ALU.subtract).then_inc(hT_done, 1)

            steps = {"XT": xt_lo_part, "PAR": params, "SCAN": scans, "COLS": columns, "ROWMAX": row_max,
                     "ARGS": exp_args, "E": split_e, "PC": split_pc, "USUM": split_usum, "DSUM": row_scale,
                     "U": split_u, "LN": row_stats, "RSTD": row_rstd, "H": normalise}

            def split_y(b, k):
                dve.wait_ge(silu_done, b * NF + (k + 1))
                if k >= 2 or not (isinstance(b, int) and b == 0):
                    dve.wait_ge(fc2_done, b * NF + (k - 1))
                v.tensor_copy(y_hi[k % 2][:], y_f[k % 2][:]).then_inc(yhi_done, 1)
                dve.wait_ge(yhi_done, b * NF + (k + 1))
                v.tensor_tensor(y_lo[k % 2][:], y_f[k % 2][:], f32(y_hi[k % 2][:]), ALU.subtract).then_inc(split_done, 1)

            def finish(b, p):
                dve.wait_ge(fc2_done, b * NF + NF)
                for r in range(NJ):
                    dve.wait_ge(bias_added, b * NJ + (r + 1))
                    v.tensor_tensor(xt[p][:, r, :], z_ps[r][:], xt[p][:, r, :], ALU.add).then_inc(final_done, 1)

            def ffn(b, p, with_a):
                ch = Chain(b + 1)
                split_y(b, 0)
                for h in range(2 * NF - 3):
                    if h % 2 == 0:
                        split_y(b, h // 2 + 1)
                    if with_a:
                        for name, n in DVE_PLAN.get(h, []):
                            steps[name](b + 1, n, 1 - p, ch)
                if with_a:
                    assert ch.n == A_STEPS, ch.n
                    for c in range(ND):
                        h_lo_part(b + 1, c)
                finish(b, p)

            def prep(i, j, hi, lo, scale):
                q = stage_q[j]
                dve.wait_ge(q_in[j], i * 16 + 16)
                dve.wait_ge(s_in[j], i * 16 + 16)
                v.scalar_tensor_tensor(q, q.bitcast(I32), -128.0, stage_s[j][:], ALU.add, ALU.mult).then_inc(wf_ready, 1)
                dve.wait_ge(wf_ready, i * 4 + (j + 1))
                v.tensor_scalar(stage_s[j][:], q, scale, None, ALU.mult).then_inc(wg_ready, 1)
                dve.wait_ge(whi_ready, i * 4 + (j + 1))
                v.tensor_tensor(lo, stage_s[j][:], f32(hi), ALU.subtract).then_inc(w_ready, 1)

            ch = Chain(0)
            for name, n in in_order(DVE_PLAN):
                steps[name](0, n, 0, ch)
            for c in range(ND):
                h_lo_part(0, c)
            flat = [t[:].rearrange("p c f -> p (c f)") for t in (w1_hi, w1_lo, w2_hi, w2_lo)]
            with dve.Fori(0, ND) as i:
                for j in range(NQ):
                    at = bass.ds(i * F + j * UNIT, UNIT)
                    prep(i, j, flat[0][:, at], flat[1][:, at], gam[:, bass.ds(i, 1)])
            dve.wait_ge(beta_done, ND * NQ)
            link(v.tensor_reduce(b1x[:], y_ps[0][:, 0:ND * NF].rearrange("p (c k) -> p k c", c=ND), AX_X, ALU.add))
            v.tensor_tensor(b1[:], b1[:], b1x[:], ALU.add).then_inc(b1_ready, 1)
            with dve.Fori(0, NF // 4) as i:
                for j in range(4):
                    at = bass.ds((i * 4 + j) * D, D)
                    prep(i + ND, j, flat[2][:, at], flat[3][:, at], 0.5)
            ffn(0, 0, True)
            ffn(1, 1, True)
            with dve.Fori(1, B // 2 - 1) as i:
                ffn(i * 2, 0, True)
                ffn(i * 2 + 1, 1, True)
            ffn(B - 2, 0, True)
            ffn(B - 1, 1, False)

        @block.tensor
        def _(pe):
            mm = nc.tensor.matmul

            def transpose_x(a, s, p):
                pe.wait_ge(x_in[s], a * 16 + 16)
                if s:
                    pe.wait_ge(xt_ready, a * NJ + s)
                elif not isinstance(a, int):
                    pe.wait_ge(hT_done, a * ND - 1)
                for c in range(ND):
                    last = nc.tensor.transpose(a_ps[0][:, c * P:(c + 1) * P], xt[p][:, s, c * P:(c + 1) * P], ident[:])
                last.then_inc(xt_tr, 1)

            def project(a, s, p):
                pe.wait_ge(xt_ready, a * NJ + (s + 1))
                if s == 0 and not isinstance(a, int):
                    pe.wait_ge(hT_done, a * ND)
                o = a_ps[1][:, s * P:(s + 1) * P]
                for c in range(ND):
                    cols = slice(c * P, (c + 1) * P)
                    mm(o, wc_hi[:, c, :], part_hi[:, cols], start=(c == 0), stop=False)
                    mm(o, wc_hi[:, c, :], part_lo[:, cols], start=False, stop=False)
                    last = mm(o, wc_lo[:, c, :], part_hi[:, cols], start=False, stop=(c == ND - 1))
                last.then_inc(at_done, 1)

            def scores(a, _, p):
                pe.wait_ge(tanh_done, a + 1)
                mm(a_ps[0][:], v_bc[:], th, start=True, stop=True).then_inc(sc_mm, 1)

            def u_sum(a, L, p):
                if L == 0:
                    pe.wait_ge(e_ready, a + 1)
                pe.wait_ge(xs_ready, a * 8 + (L + 1))
                mm(a_ps[0][:], e_cols[:, L, :], xs_hi[:], start=(L == 0), stop=False)
                mm(a_ps[0][:], e_cols[:, L, :], xs_lo[:], start=False, stop=(L == NJ - 1)).then_inc(xs_used, 1)

            def e_sums(a, _, p):
                for L in range(NJ):
                    last = mm(a_ps[1][:, 0:2], e_cols[:, L, :], ones2[:], start=(L == 0), stop=(L == NJ - 1))
                last.then_inc(usum_done, 1)

            def p_sums(a, _, p):
                pe.wait_ge(pc_ready, a + 1)
                pe.wait_ge(usum_ready, a + 1)
                for J in range(NJ):
                    o, cols = a_ps[1][:, 2 + 2 * J:4 + 2 * J], slice(J * P, (J + 1) * P)
                    mm(o, part_hi[:, cols], ones2[:], start=True, stop=False)
                    mm(o, part_lo[:, cols], ones2[:], start=False, stop=False)
                    mm(o, coef_hi[:, cols], u_sums[:], start=False, stop=False)
                    last = mm(o, coef_lo[:, cols], u_sums[:], start=False, stop=True)
                last.then_inc(dsum_done, 1)

            def pool_block(a, J, p):
                o, cols = a_ps[J % 2][:], slice(J * P, (J + 1) * P)
                if J == 0:
                    pe.wait_ge(u_ready, a + 1)
                elif J == 1:
                    pe.wait_ge(c_ready, a + 1)
                else:
                    pe.wait_ge(pooled_done, a * NJ + (J - 1))
                pe.wait_ge(xs_ready, a * 8 + (NJ + J + 1))
                mm(o, part_hi[:, cols], xs_hi[:], start=True, stop=False)
                mm(o, part_hi[:, cols], xs_lo[:], start=False, stop=False)
                mm(o, part_lo[:, cols], xs_hi[:], start=False, stop=False).then_inc(xs_used, 1)
                mm(o, coef_hi[:, cols], u_rows[:], start=False, stop=False)
                mm(o, coef_lo[:, cols], u_rows[:], start=False, stop=True).then_inc(pz_done, 1)

            def transpose_h(a, c):
                if c == 0:
                    pe.wait_ge(h_ready, a * NJ + NJ)
                if c >= 2:
                    pe.wait_ge(hT_done, a * ND + (c - 1))
                for J in range(NJ):
                    last = nc.tensor.transpose(a_ps[c % 2][:, J * P:(J + 1) * P], pooled[J][:, c * P:(c + 1) * P], ident[:])
                last.then_inc(h_tr, 1)

            steps = {"T": transpose_x, "AT": project, "SC": scores, "U": u_sum, "USUM": e_sums, "DSUM": p_sums,
                     "PZ": pool_block}

            def fc1(b, k):
                if k < 2:
                    pe.wait_ge(hT_done, b * ND + ND)
                if k >= 2 or not (isinstance(b, int) and b == 0):
                    pe.wait_ge(silu_done, b * NF + (k - 1))
                o, cols = y_ps[k % 2][:], slice(k * P, (k + 1) * P)
                for c in range(ND):
                    mm(o, w1_hi[:, c, cols], hT_hi[:, c, :], start=(c == 0), stop=False)
                    mm(o, w1_hi[:, c, cols], hT_lo[:, c, :], start=False, stop=False)
                    last = mm(o, w1_lo[:, c, cols], hT_hi[:, c, :], start=False, stop=(c == ND - 1))
                last.then_inc(fc1_done, 1)

            def fc2(b, k):
                pe.wait_ge(split_done, b * NF + (k + 1))
                if k == 0:
                    pe.wait_ge(final_done, b * NJ)
                for r in range(NJ):
                    rows = slice(r * P, (r + 1) * P)
                    mm(z_ps[r][:], y_hi[k % 2][:, rows], w2_hi[:, k, :], start=(k == 0), stop=False)
                    mm(z_ps[r][:], y_hi[k % 2][:, rows], w2_lo[:, k, :], start=False, stop=False)
                    last = mm(z_ps[r][:], y_lo[k % 2][:, rows], w2_hi[:, k, :], start=False, stop=(k == NF - 1))
                last.then_inc(fc2_done, 1)

            def ffn(b, p, with_a):
                for h in range(LAST):
                    if h % 2 == 0:
                        fc1(b, h // 2 + 2)
                    else:
                        fc2(b, h // 2)
                    if with_a:
                        for name, n in PE_PLAN.get(h, []):
                            steps[name](b + 1, n, 1 - p)
                if with_a:
                    transpose_h(b + 1, 0)
                    transpose_h(b + 1, 1)
                fc2(b, NF - 2)
                if with_a:
                    transpose_h(b + 1, 2)
                    transpose_h(b + 1, 3)
                fc2(b, NF - 1)
                if with_a:
                    fc1(b + 1, 0)
                    fc1(b + 1, 1)

            pe.wait_ge(consts_ready, 1)
            pe.wait_ge(pool_const, POOL_CONSTS)
            for name, n in in_order(PE_PLAN):
                steps[name](0, n, 0)
            for c in range(ND):
                transpose_h(0, c)
            with pe.Fori(0, ND) as i:
                for j in range(NQ):
                    pe.wait_ge(wf_ready, i * 4 + (j + 1))
                    for t in range(UNIT // P):
                        last = mm(y_ps[0][:, bass.ds(i * NF + (j * 4 + t), 1)], stage_q[j][:, t * P:(t + 1) * P],
                                  bet[:, bass.ds(i, 1)], start=True, stop=True)
                    last.then_inc(beta_done, 1)
            pe.wait_ge(w_ready, NPREP)
            pe.wait_ge(b1_ready, 1)
            fc1(0, 0)
            fc1(0, 1)
            ffn(0, 0, True)
            ffn(1, 1, True)
            with pe.Fori(1, B // 2 - 1) as i:
                ffn(i * 2, 0, True)
                ffn(i * 2 + 1, 1, True)
            ffn(B - 2, 0, True)
            ffn(B - 1, 1, False)


_INS = ['x', 'itok_B_0_2', 'L0_cond_W1', 'L0_cond_b1', 'L0_cond_v', 'L0_ffn_ln_gamma', 'L0_ffn_ln_beta',
        'L0_ffn_fc1_q', 'L0_ffn_fc1_scales', 'L0_ffn_fc1_bias', 'L0_ffn_fc2_q', 'L0_ffn_fc2_scales',
        'L0_ffn_fc2_bias']


def kernel(**inputs):
    import numpy as _np
    import concourse.bacc as _bacc
    from concourse import mybir as _mybir
    from concourse.bass_utils import run_bass_kernel_spmd as _run

    nc = _bacc.Bacc("TRN2", target_bir_lowering=False, num_devices=1)
    arrays, args = {}, []
    for name in _INS:
        a = _np.ascontiguousarray(inputs[name])
        arrays[f"in_{name}_dram"] = a
        args.append(nc.dram_tensor(f"in_{name}_dram", a.shape, _mybir.dt.from_np(a.dtype), kind="ExternalInput").ap())
    shape = arrays["in_x_dram"].shape
    args.append(nc.dram_tensor("out_0_dram", shape, _mybir.dt.float32, kind="ExternalOutput").ap())
    build(nc, *args)
    r = _run(nc, [arrays], core_ids=[0])
    return r.results[0]["out_0_dram"]
```

```python
from contextlib import ExitStack

import concourse.bass as bass
from concourse import mybir

ALU = mybir.AluOpType
ACT = mybir.ActivationFunctionType
AX_X = mybir.AxisListType.X
F32 = mybir.dt.float32
F32R = mybir.dt.float32r
I32 = mybir.dt.int32

P = 128
NEG = -1e30
EPS = 1e-5


def build(nc, x, itok, cond_w, cond_b, cond_v, gamma, beta, fc1_q, fc1_s, fc1_b, fc2_q, fc2_s, fc2_b, out):
    B, S, D = x.shape
    F = fc1_q.shape[1]
    NJ = S // P
    ND = D // P
    NF = F // P
    NG = NF // ND
    assert cond_w.shape == [D, P] or tuple(cond_w.shape) == (D, P)
    assert S == 512 and D == 512 and NJ == 4 and ND == 4 and NF == 16 and B % 2 == 0
    SLOT = 514
    POOL_CONSTS = 26
    A_STEPS = 49

    with ExitStack() as ctx:
        def sb(name, shape, dt=F32):
            return ctx.enter_context(nc.sbuf_tensor(name, shape, dt))

        def sem(name):
            return ctx.enter_context(nc.semaphore(name))

        with ExitStack() as raw:
            q1, s1, q2, s2 = (raw.enter_context(nc.sbuf_tensor(name, shape, dt)) for name, shape, dt in (
                ("fc1_codes", [P, ND, F], I32), ("fc1_scaled", [P, ND, F], F32),
                ("fc2_codes", [P, NF, D], I32), ("fc2_scaled", [P, NF, D], F32)))
        w1_hi = sb("w1_hi", [P, ND, F], F32R)
        w1_lo = sb("w1_lo", [P, ND, F], F32R)
        w2_hi = sb("w2_hi", [P, NF, D], F32R)
        w2_lo = sb("w2_lo", [P, NF, D], F32R)
        wc_hi = sb("wc_hi", [P, ND, P], F32R)
        wc_lo = sb("wc_lo", [P, ND, P], F32R)
        hT_hi = sb("hT_hi", [P, ND, S], F32R)
        hT_lo = sb("hT_lo", [P, ND, S], F32R)
        xt = [sb(f"x{p}", [P, NJ, D]) for p in range(2)]
        scratch = sb("scratch", [P, NJ * SLOT])
        xs_hi = sb("xs_hi", [P, D], F32R)
        xs_lo = sb("xs_lo", [P, D], F32R)
        part_hi = sb("part_hi", [P, S], F32R)
        part_lo = sb("part_lo", [P, S], F32R)
        coef_hi = sb("coef_hi", [P, S], F32R)
        coef_lo = sb("coef_lo", [P, S], F32R)
        e_cols = sb("e_cols", [P, NJ, P], F32R)
        u_rows = sb("u_rows", [P, D], F32R)
        u_sums = sb("u_sums", [P, P], F32R)
        y_f = [sb(f"y_f{i}", [P, S]) for i in range(2)]
        y_hi = [sb(f"y_hi{i}", [P, S], F32R) for i in range(2)]
        y_lo = [sb(f"y_lo{i}", [P, S], F32R) for i in range(2)]
        b2h = sb("b2h", [P, D])
        ident = sb("ident", [P, P])
        v_bc = sb("v_bc", [P, P])
        sgn = sb("sgn", [P, P])
        sgn_blk = sb("sgn_blk", [P, NJ])
        pen_sel = sb("pen_sel", [P, NJ])
        pen_own = sb("pen_own", [P, NJ])
        ones = sb("ones", [P, P], F32R)
        b1c = sb("b1c", [P, 1])
        v_col = sb("v_col", [P, 1])
        gam = sb("gam", [P, ND])
        bet = sb("bet", [P, ND])
        b1 = sb("b1", [P, NF])
        b1x = sb("b1x", [P, NF])
        tok_i = sb("tok_i", [P, B], I32)
        tok = sb("tok", [P, B])
        is0 = sb("is0", [P, B])
        is1 = sb("is1", [P, B])
        row_i = sb("row_i", [P, NJ], I32)
        row_f = sb("row_f", [P, NJ])
        row_a = sb("row_a", [P, NJ])
        row_b = sb("row_b", [P, NJ])
        par = sb("par", [P, B, 8])
        cur = sb("cur", [P, 8])
        pen_p = sb("pen_p", [P, P])
        columns4 = sb("columns4", [P, 14 * NJ])
        taken = iter(range(14))

        def small():
            k = next(taken)
            return columns4[:, k * NJ:(k + 1) * NJ]

        pen_c = small()
        blk_max = small()
        s_col = small()
        e_arg = small()
        e_f = small()
        m_sel = small()
        m_col = sb("m_col", [P, 1])
        dcnt = small()
        c_row = small()
        stats = sb("stats", [P, NJ, 6])
        mv = sb("mv", [P, NJ, 2])
        ve = small()
        nt = small()
        rs_i = small()
        one_col = small()
        rstd = [small() for _ in range(2)]

        th = scratch[:, 0:S]
        sc_row = scratch[:, SLOT:SLOT + S]
        fwd = scratch[:, 2 * SLOT:2 * SLOT + S + 1]
        bwd = scratch[:, 3 * SLOT:3 * SLOT + S + 1]
        p_f = scratch[:, 2 * SLOT:2 * SLOT + S]
        c_f = scratch[:, 3 * SLOT:3 * SLOT + S]
        pooled = [scratch[:, J * SLOT:J * SLOT + D] for J in range(NJ)]
        wc_f = scratch[:, SLOT:SLOT + ND * P]

        def by_block(ap):
            return ap.rearrange("p (j n) -> p j n", j=NJ)

        def f32(ap):
            return ap.bitcast(F32)

        def bank(name):
            return ctx.enter_context(nc.psum_tensor(name, [P, 512], F32))

        z_ps = [bank(f"z_ps{r}") for r in range(NJ)]
        y_ps = [bank(f"y_ps{i}") for i in range(2)]
        a_ps = [bank(f"a_ps{i}") for i in range(2)]

        const_in = sem("const_in")
        bias_in = sem("bias_in")
        x_in = [[sem(f"x_in{p}_{J}") for J in range(NJ)] for p in range(2)]
        stored = [sem(f"stored{J}") for J in range(NJ)]
        pool_const = sem("pool_const")
        pool_step = sem("pool_step")
        dve_const = sem("dve_const")
        dve_step = sem("dve_step")
        consts_ready = sem("consts_ready")
        w_in = [sem(f"w_in{g}") for g in range(2 * ND)]
        wf_ready = sem("wf_ready")
        whi_ready = sem("whi_ready")
        w_ready = sem("w_ready")
        beta_done = sem("beta_done")
        b1_ready = sem("b1_ready")
        xt_tr = sem("xt_tr")
        xt_hi = sem("xt_hi")
        xt_ready = sem("xt_ready")
        at_done = sem("at_done")
        tanh_done = sem("tanh_done")
        sc_mm = sem("sc_mm")
        sc_ready = sem("sc_ready")
        args_ready = sem("args_ready")
        exp_done = sem("exp_done")
        e_ready = sem("e_ready")
        pc_ready = sem("pc_ready")
        xs_ready = sem("xs_ready")
        xs_used = sem("xs_used")
        usum_done = sem("usum_done")
        usum_ready = sem("usum_ready")
        dsum_done = sem("dsum_done")
        c_ready = sem("c_ready")
        u_hi = sem("u_hi")
        u_ready = sem("u_ready")
        pz_done = sem("pz_done")
        pooled_done = sem("pooled_done")
        res_added = sem("res_added")
        bias_added = sem("bias_added")
        h_ready = sem("h_ready")
        h_tr = sem("h_tr")
        hT_hi_done = sem("hT_hi_done")
        hT_done = sem("hT_done")
        fc1_done = sem("fc1_done")
        silu_done = sem("silu_done")
        yhi_done = sem("yhi_done")
        split_done = sem("split_done")
        fc2_done = sem("fc2_done")
        final_done = sem("final_done")

        LAST = 2 * NF - 4
        PE_PLAN = {3: [("T", 0)], 4: [("AT", 0), ("T", 1)], 5: [("AT", 1), ("T", 2)], 6: [("AT", 2), ("T", 3)],
                   7: [("AT", 3)], 8: [("SC", 0)], 13: [("U", 0)], 14: [("U", 1), ("USUM", 0)], 15: [("U", 2)],
                   16: [("U", 3), ("DSUM", 0)], 17: [("PZ", 0)], 18: [("PZ", 1)], 19: [("PZ", 2)], 20: [("PZ", 3)]}
        ACT_PLAN = {3: [("XT", 0)], 4: [("XT", 1)], 5: [("XT", 2)], 6: [("XT", 3)], 7: [("TANH", 0)],
                    8: [("SC", 0)], 12: [("EXP", 0)], 16: [("U", 0)], 17: [("PZ", 0)], 18: [("PZ", 1)],
                    19: [("PZ", 2)], 20: [("PZ", 3)]}
        DVE_PLAN = {3: [("XT", 0)], 4: [("XT", 1)], 5: [("XT", 2)], 6: [("XT", 3)], 7: [("PAR", 0)],
                    8: [("SCAN", 0)], 9: [("COLS", 0)], 10: [("ROWMAX", 0)], 11: [("ARGS", 0)], 12: [("E", 0)],
                    13: [("PC", 0)], 14: [("USUM", 0)], 16: [("DSUM", 0), ("U", 0)], 17: [("LN", 0)],
                    18: [("LN", 1)], 19: [("LN", 2)], 20: [("LN", 3)], 21: [("RSTD", 0)], 22: [("H", 0)]}

        def in_order(plan, units=()):
            out = list(dict(units).get("first", []))
            for h in sorted(plan):
                for step in plan[h]:
                    out += [step] + list(dict(units).get(step, []))
            return out

        DVE_UNITS = {("XT", 3): [("D", 0)], ("ARGS", 0): [("D", 1), ("D", 2)], ("PC", 0): [("L", 0), ("D", 3)],
                     ("DSUM", 0): [("L", 1)], ("U", 0): [("L", 2)], ("LN", 0): [("D", 4)], ("LN", 1): [("L", 3)],
                     ("LN", 2): [("D", 5)]}
        ACT_UNITS = {("SC", 0): [("H", 0)], ("EXP", 0): [("H", 1), ("H", 2)], ("U", 0): [("H", 3)],
                     ("PZ", 2): [("H", 4)], ("PZ", 3): [("H", 5)]}
        DVE_LATE = {0: [("L", 5)], 1: [("D", 6)], 2: [("D", 7)], 4: [("L", 6)], 5: [("L", 7)]}
        ACT_LATE = {2: [("H", 6)], 3: [("H", 7)]}
        PE_UNITS = {("SC", 0): [("B", 0), ("B", 1), ("B", 2)], ("U", 3): [("B", 3)]}

        block = ctx.enter_context(nc.Block())

        @block.sync
        def _(sp):
            x_dram = x.rearrange("b (j p) d -> (b j) p d", p=P)
            out_dram = out.rearrange("b (j p) d -> (b j) p d", p=P)

            def load_x(a, p):
                for J in range(NJ):
                    sp.dma_start(xt[p][:, J, :], x_dram[bass.ds(a * NJ + J, 1), :, :].rearrange("a p d -> p (a d)")).then_inc(x_in[p][J], 16)

            def store(b, p, J):
                sp.wait_ge(final_done, b * NJ + (J + 1))
                sp.dma_start(out_dram[bass.ds(b * NJ + J, 1), :, :].rearrange("a p d -> p (a d)"), xt[p][:, J, :]).then_inc(stored[J], 16)

            load_x(0, 0)
            sp.dma_start(wc_f.rearrange("p (c a) -> p c a", c=ND), cond_w.rearrange("(c p) a -> p c a", p=P)).then_inc(const_in, 16)
            sp.dma_start(b1c[:], cond_b.rearrange("(p o) -> p o", o=1)).then_inc(const_in, 16)
            sp.dma_start(v_col[:], cond_v.rearrange("(p o) -> p o", o=1)).then_inc(const_in, 16)
            sp.dma_start(gam[:], gamma.rearrange("(c p) -> p c", p=P), allow_slow_non_contiguous=True).then_inc(const_in, 16)
            sp.dma_start(bet[:], beta.rearrange("(c p) -> p c", p=P), allow_slow_non_contiguous=True).then_inc(const_in, 16)
            sp.dma_start(b1x[:], fc1_b.rearrange("(c p) -> p c", p=P), allow_slow_non_contiguous=True).then_inc(const_in, 16)
            sp.dma_start(b2h[:], fc2_b.rearrange("(o d) -> o d", o=1).to_broadcast([P, D])).then_inc(bias_in, 16)
            sp.dma_start(tok_i[:], itok.rearrange("(o d) -> o d", o=1).to_broadcast([P, B])).then_inc(const_in, 16)

            for c in range(ND):
                sp.dma_start(q1[:, c, :], fc1_q[c * P:(c + 1) * P, :]).then_inc(w_in[c], 16)
                sp.dma_start(s1[:, c, :], fc1_s[c:c + 1, :].to_broadcast([P, F])).then_inc(w_in[c], 16)
            for g in range(ND):
                rows = slice(g * NG, (g + 1) * NG)
                sp.dma_start(q2[:, rows, :], fc2_q[g * NG * P:(g + 1) * NG * P, :].rearrange("(k p) d -> p k d", p=P)).then_inc(w_in[ND + g], 16)
                sp.dma_start(s2[:, rows, :], fc2_s[rows, :].rearrange("(o k) d -> o k d", o=1).to_broadcast([P, NG, D])).then_inc(w_in[ND + g], 16)
            load_x(1, 1)

            def turn(b, p):
                for J in range(NJ):
                    store(b - 1, p, J)
                for J in range(NJ):
                    sp.wait_ge(stored[J], b * 16)
                    sp.dma_start(xt[p][:, J, :], x_dram[bass.ds((b + 1) * NJ + J, 1), :, :].rearrange("a p d -> p (a d)")).then_inc(x_in[p][J], 16)

            with sp.Fori(0, B // 2 - 1) as i:
                turn(i * 2 + 1, 0)
                turn(i * 2 + 2, 1)
            for b in (B - 2, B - 1):
                for J in range(NJ):
                    store(b, b % 2, J)
            for J in range(NJ):
                sp.wait_ge(stored[J], 16 * B)

        @block.gpsimd
        def _(pool):
            done = [0]

            def link(ins):
                done[0] += 1
                ins.then_inc(pool_const, 1)
                pool.wait_ge(pool_const, done[0])

            link(nc.gpsimd.memset(ident[:], 0.0))
            link(nc.gpsimd.affine_select(out=ident[:], in_=ident[:], compare_op=ALU.not_equal, fill=1.0, base=0,
                                         pattern=[[-1, P]], channel_multiplier=1))
            link(nc.gpsimd.memset(sgn[:], 0.0))
            link(nc.gpsimd.affine_select(out=sgn[:], in_=sgn[:], compare_op=ALU.is_ge, fill=1.0, base=0,
                                         pattern=[[-1, P]], channel_multiplier=1))
            link(nc.gpsimd.affine_select(out=sgn[:], in_=sgn[:], compare_op=ALU.is_ge, fill=-1.0, base=0,
                                         pattern=[[1, P]], channel_multiplier=-1))
            link(nc.gpsimd.memset(sgn_blk[:], 0.0))
            link(nc.gpsimd.memset(pen_sel[:], 0.0))
            link(nc.gpsimd.memset(pen_own[:], 0.0))
            for q in range(4):
                rows = slice(32 * q, 32 * q + 32)
                link(nc.gpsimd.affine_select(out=sgn_blk[rows, :], in_=sgn_blk[rows, :], compare_op=ALU.is_ge,
                                             fill=1.0, base=0, pattern=[[-1, NJ]], channel_multiplier=1))
                link(nc.gpsimd.affine_select(out=sgn_blk[rows, :], in_=sgn_blk[rows, :], compare_op=ALU.is_ge,
                                             fill=-1.0, base=0, pattern=[[1, NJ]], channel_multiplier=-1))
                link(nc.gpsimd.affine_select(out=pen_sel[rows, :], in_=pen_sel[rows, :], compare_op=ALU.is_equal,
                                             fill=NEG, base=0, pattern=[[1, NJ]], channel_multiplier=-1))
                link(nc.gpsimd.affine_select(out=pen_own[rows, :], in_=pen_own[rows, :], compare_op=ALU.not_equal,
                                             fill=NEG, base=0, pattern=[[1, NJ]], channel_multiplier=-1))
            link(nc.gpsimd.iota(row_i[:], pattern=[[P, NJ]], base=0, channel_multiplier=1))

            link(nc.gpsimd.memset(one_col, 1.0))
            assert done[0] == POOL_CONSTS

            def split_x(a, p, n):
                J = n % NJ
                if n < NJ:
                    pool.wait_ge(x_in[p][J], a * 8 + (16 - 8 * p))
                if n or not isinstance(a, int) or a:
                    pool.wait_ge(xs_used, a * 8 + n)
                nc.gpsimd.tensor_tensor(xs_hi[:], xt[p][:, J, :], one_col[:, 0:1].to_broadcast([P, D]),
                                        ALU.mult).then_inc(pool_step, 1)
                pool.wait_ge(pool_step, a * 8 + (n + 1))
                nc.gpsimd.tensor_tensor(xs_lo[:], xt[p][:, J, :], f32(xs_hi[:]), ALU.subtract).then_inc(xs_ready, 1)

            def add_bias(a, p, J):
                pool.wait_ge(res_added, a * NJ + (J + 1))
                nc.gpsimd.tensor_tensor(xt[p][:, J, :], xt[p][:, J, :], b2h[:], ALU.add).then_inc(bias_added, 1)

            def stage_a(a, p, first=False):
                for n in range(8):
                    split_x(a, p, n)
                if first:
                    pool.wait_ge(bias_in, 16)
                    link(nc.gpsimd.tensor_scalar(b2h[:], b2h[:], 0.5, None, ALU.mult))
                for J in range(NJ):
                    add_bias(a, p, J)

            stage_a(0, 0, True)
            with pool.Fori(0, B // 2 - 1) as i:
                stage_a(i * 2 + 1, 1)
                stage_a(i * 2 + 2, 0)
            stage_a(B - 1, 1)

        @block.scalar
        def _(act):
            def copy(o, i):
                return nc.scalar.activation(o, i, ACT.Copy)

            def xt_hi_part(a, s):
                act.wait_ge(xt_tr, a * NJ + (s + 1))
                if s:
                    act.wait_ge(at_done, a * NJ + s)
                copy(part_hi[:], a_ps[0][:]).then_inc(xt_hi, 1)

            def tanh(a, _):
                act.wait_ge(at_done, a * NJ + NJ)
                nc.scalar.activation(th, a_ps[1][:], ACT.Tanh, bias=b1c[:, 0:1]).then_inc(tanh_done, 1)

            def scores(a, _):
                act.wait_ge(sc_mm, a + 1)
                copy(sc_row, a_ps[0][:]).then_inc(sc_ready, 1)

            def exps(a, _):
                act.wait_ge(args_ready, a + 1)
                nc.scalar.activation(e_f[:], e_arg[:], ACT.Exp).then_inc(exp_done, 1)
                nc.scalar.activation(c_f, c_f, ACT.Exp, bias=m_col[:, 0:1]).then_inc(exp_done, 1)
                for J in range(NJ):
                    blk = p_f[:, J * P:(J + 1) * P]
                    nc.scalar.activation(blk, blk, ACT.Exp, bias=s_col[:, J:J + 1]).then_inc(exp_done, 1)

            def u_hi_part(a, _):
                act.wait_ge(xs_used, a * 8 + NJ)
                copy(u_rows[:], a_ps[0][:]).then_inc(u_hi, 1)

            def pool_rows(a, J):
                if J == 0:
                    act.wait_ge(c_ready, a + 1)
                act.wait_ge(pz_done, a * NJ + (J + 1))
                nc.scalar.activation(pooled[J], a_ps[J % 2][:], ACT.Copy, scale=c_row[:, J:J + 1]).then_inc(pooled_done, 1)

            def h_hi_part(a, c):
                if c == 0 and not (isinstance(a, int) and a == 0):
                    act.wait_ge(fc1_done, a * NF)
                act.wait_ge(h_tr, a * ND + (c + 1))
                copy(hT_hi[:, c, :], a_ps[c % 2][:]).then_inc(hT_hi_done, 1)

            steps = {"XT": xt_hi_part, "TANH": tanh, "SC": scores, "EXP": exps, "U": u_hi_part, "PZ": pool_rows}

            def silu(b, k):
                act.wait_ge(fc1_done, b * NF + (k + 1))
                if k >= 2 or not (isinstance(b, int) and b == 0):
                    act.wait_ge(split_done, b * NF + (k - 1))
                nc.scalar.activation(y_f[k % 2][:], y_ps[k % 2][:], ACT.Silu, bias=b1[:, k:k + 1]).then_inc(silu_done, 1)

            def w_hi_part(g, _):
                act.wait_ge(wf_ready, g + 1)
                if g < ND:
                    nc.scalar.activation(w1_hi[:, g, :], s1[:, g, :], ACT.Copy, scale=gam[:, g:g + 1]).then_inc(whi_ready, 1)
                else:
                    rows = slice((g - ND) * NG, (g - ND + 1) * NG)
                    nc.scalar.activation(w2_hi[:, rows, :], s2[:, rows, :], ACT.Copy, scale=0.5).then_inc(whi_ready, 1)

            def ffn(b, with_a, first=False):
                for k in range(2):
                    if first:
                        silu(b, k)
                    else:
                        act.wait_ge(fc1_done, b * NF + (k + 1))
                        act.wait_ge(split_done, b * NF + (k - 1))
                        nc.scalar.activation(y_f[k % 2][:], y_ps[k % 2][:], ACT.Silu,
                                             bias=b1[:, k:k + 1]).then_inc(silu_done, 1)
                for h in range(LAST):
                    if h % 2 == 0:
                        silu(b, h // 2 + 2)
                    if first:
                        for _, g in ACT_LATE.get(h, []):
                            w_hi_part(g, 0)
                    if with_a:
                        for name, n in ACT_PLAN.get(h, []):
                            steps[name](b + 1, n)
                if with_a:
                    for c in range(ND):
                        h_hi_part(b + 1, c)

            act.wait_ge(consts_ready, 1)
            for name, n in in_order(ACT_PLAN, ACT_UNITS):
                if name == "H":
                    w_hi_part(n, 0)
                else:
                    steps[name](0, n)
            for c in range(ND):
                h_hi_part(0, c)
            act.wait_ge(b1_ready, 1)
            ffn(0, True, True)
            ffn(1, True)
            with act.Fori(1, B // 2 - 1) as i:
                ffn(i * 2, True)
                ffn(i * 2 + 1, True)
            ffn(B - 2, True)
            ffn(B - 1, False)

        @block.vector
        def _(dve):
            v = nc.vector
            done = [0]

            def link(ins):
                done[0] += 1
                ins.then_inc(dve_const, 1)
                dve.wait_ge(dve_const, done[0])

            link(v.memset(f32(e_cols[:]), 0.0))
            link(v.memset(f32(ones[:]), 1.0))
            dve.wait_ge(const_in, 16 * 7)
            link(v.tensor_copy(v_bc[:], v_col[:, 0:1].to_broadcast([P, P])))
            wc_flat = [t[:].rearrange("p c a -> p (c a)") for t in (wc_hi, wc_lo)]
            link(v.tensor_copy(wc_flat[0], wc_f))
            link(v.tensor_tensor(wc_flat[1], wc_f, f32(wc_flat[0]), ALU.subtract))
            link(v.tensor_copy(tok[:], tok_i[:]))
            link(v.tensor_scalar(is0[:], tok[:], 0.0, None, ALU.is_equal))
            link(v.tensor_scalar(is1[:], tok[:], 1.0, None, ALU.is_equal))
            link(v.tensor_tensor(par[:, :, 0], is1[:], is0[:], ALU.subtract))
            link(v.tensor_scalar(par[:, :, 1], tok[:], 0.0, NEG, ALU.not_equal, ALU.mult))
            link(v.tensor_scalar(par[:, :, 2], tok[:], 1.0, NEG, ALU.not_equal, ALU.mult))
            link(v.tensor_scalar(par[:, :, 3], par[:, :, 0], 0.0, NEG, ALU.not_equal, ALU.mult))
            dve.wait_ge(pool_const, POOL_CONSTS)
            link(v.tensor_copy(row_f[:], row_i[:]))
            link(v.tensor_scalar(row_a[:], row_f[:], float(S - 2), None, ALU.subtract))
            link(v.tensor_scalar(row_b[:], row_f[:], -1.0, 1.0, ALU.mult, ALU.add))
            for J in range(NJ):
                cnt = par[:, :, 4 + J]
                link(v.tensor_scalar(cnt, is0[:], row_a[:, J:J + 1], float(S - 1), ALU.mult, ALU.add))
                link(v.scalar_tensor_tensor(cnt, is1[:], row_b[:, J:J + 1], cnt, ALU.mult, ALU.add))
            v.tensor_copy(b1[:], b1x[:]).then_inc(consts_ready, 1)

            class Chain:
                def __init__(self, a):
                    self.base, self.n = a * A_STEPS, 0

                def __call__(self, ins):
                    self.n += 1
                    ins.then_inc(dve_step, 1)
                    dve.wait_ge(dve_step, self.base + self.n)

            def xt_lo_part(a, s, p, ch):
                dve.wait_ge(xt_hi, a * NJ + (s + 1))
                v.tensor_tensor(part_lo[:], a_ps[0][:], f32(part_hi[:]), ALU.subtract).then_inc(xt_ready, 1)

            def params(a, _, p, ch):
                flat = par[:].rearrange("p b k -> p (b k)")
                ch(v.tensor_copy(cur[:], flat[:, bass.ds(a * 8, 8)]))
                ch(v.tensor_scalar(pen_p[:], sgn[:], cur[:, 0:1], NEG, ALU.is_equal, ALU.mult))
                ch(v.tensor_scalar(pen_c[:], sgn_blk[:], cur[:, 0:1], NEG, ALU.is_equal, ALU.mult))
                ch(v.tensor_tensor(pen_c[:], pen_c[:], pen_own[:], ALU.min))

            def scans(a, _, p, ch):
                dve.wait_ge(sc_ready, a + 1)
                ch(v.memset(fwd[:, 0:1], NEG))
                ch(v.memset(bwd[:, S:S + 1], NEG))
                ch(v.tensor_tensor_scan(fwd[:, 1:S + 1], sc_row, sc_row, NEG, ALU.max, ALU.max))
                ch(v.tensor_tensor_scan(bwd[:, 0:S][:, ::-1], sc_row[:, ::-1], sc_row[:, ::-1], NEG, ALU.max, ALU.max))

            def columns(a, _, p, ch):
                ch(v.tensor_reduce(blk_max[:], by_block(sc_row), AX_X, ALU.max))
                ch(v.tensor_tensor(by_block(th), by_block(sc_row), ident[:].rearrange("p (o n) -> p o n", o=1).to_broadcast([P, NJ, P]), ALU.mult))
                ch(v.tensor_reduce(s_col[:], by_block(th), AX_X, ALU.add))
                ch(v.tensor_tensor(e_arg[:], s_col[:], blk_max[:], ALU.subtract))
                ch(v.tensor_tensor(m_sel[:], blk_max[:], pen_sel[:], ALU.add))
                ch(v.tensor_reduce(m_col[:], m_sel[:], AX_X, ALU.max))

            def row_max(a, _, p, ch):
                ch(v.tensor_tensor(th, fwd[:, 0:S], bwd[:, 1:S + 1], ALU.max))
                ch(v.tensor_scalar(sc_row, fwd[:, 1:S + 1], cur[:, 1:2], None, ALU.add))
                ch(v.scalar_tensor_tensor(sc_row, bwd[:, 0:S], cur[:, 2:3], sc_row, ALU.add, ALU.max))
                ch(v.scalar_tensor_tensor(sc_row, th, cur[:, 3:4], sc_row, ALU.add, ALU.max))

            def exp_args(a, _, p, ch):
                ch(v.tensor_tensor(by_block(p_f), pen_p[:].rearrange("p (o n) -> p o n", o=1).to_broadcast([P, NJ, P]), by_block(sc_row), ALU.subtract))
                v.tensor_tensor(by_block(c_f), pen_c[:].rearrange("p (n o) -> p n o", o=1).to_broadcast([P, NJ, P]), by_block(sc_row),
                                ALU.subtract).then_inc(args_ready, 1)

            def split_e(a, _, p, ch):
                dve.wait_ge(exp_done, a * 6 + 1)
                flat = e_cols[:].rearrange("p l m -> p (l m)")

                def diag(q):
                    return flat[:, 32 * q:32 * q + (NJ - 1) * (P + 1) + 1:P + 1]
                ch(v.tensor_copy(diag(0), e_f[:]))
                ch(v.tensor_copy(diag(2), e_f[:]))
                ch(v.tensor_tensor(diag(1), e_f[:], f32(diag(0)), ALU.subtract))
                v.tensor_tensor(diag(3), e_f[:], f32(diag(0)), ALU.subtract).then_inc(e_ready, 1)

            def split_pc(a, _, p, ch):
                dve.wait_ge(exp_done, a * 6 + 6)
                ch(v.tensor_copy(part_hi[:], p_f))
                ch(v.tensor_tensor(part_lo[:], p_f, f32(part_hi[:]), ALU.subtract))
                ch(v.tensor_copy(coef_hi[:], c_f))
                v.tensor_tensor(coef_lo[:], c_f, f32(coef_hi[:]), ALU.subtract).then_inc(pc_ready, 1)

            def split_usum(a, _, p, ch):
                dve.wait_ge(usum_done, a + 1)
                ch(v.tensor_copy(u_sums[:], a_ps[1][:, 0:P]))
                v.tensor_tensor(u_sums[64:, :], a_ps[1][64:, 0:P], f32(u_sums[64:, :]), ALU.subtract).then_inc(usum_ready, 1)

            def row_scale(a, _, p, ch):
                dve.wait_ge(dsum_done, a + 1)
                ch(v.tensor_tensor(by_block(th), by_block(a_ps[1][:]), ident[:].rearrange("p (o n) -> p o n", o=1).to_broadcast([P, NJ, P]), ALU.mult))
                ch(v.tensor_reduce(dcnt[:], by_block(th), AX_X, ALU.add))
                ch(v.tensor_tensor(dcnt[:], dcnt[:], cur[:, 4:4 + NJ], ALU.mult))
                v.reciprocal(c_row[:], dcnt[:]).then_inc(c_ready, 1)

            def split_u(a, _, p, ch):
                dve.wait_ge(u_hi, a + 1)
                v.tensor_tensor(u_rows[64:, :], a_ps[0][64:, :], f32(u_rows[64:, :]), ALU.subtract).then_inc(u_ready, 1)

            def row_stats(a, J, p, ch):
                dve.wait_ge(pooled_done, a * NJ + (J + 1))
                ch(v.bn_stats(stats[:, J, :], pooled[J]))
                dve.wait_ge(xs_ready, a * 8 + (NJ + J + 1))
                v.tensor_tensor(xt[p][:, J, :], xt[p][:, J, :], pooled[J], ALU.add).then_inc(res_added, 1)
                ch(v.bn_aggr(mv[:, J, :], stats[:, J, :]))

            def row_rstd(a, _, p, ch):
                ch(v.tensor_scalar(ve[:], mv[:, :, 1], EPS, None, ALU.add))
                ch(v.tensor_scalar(rs_i[:].bitcast(I32), ve[:].bitcast(I32), 1, None, ALU.logical_shift_right))
                ch(v.tensor_scalar(rstd[0][:].bitcast(I32), rs_i[:].bitcast(I32), -1.0, float(0x5f3759df), ALU.mult, ALU.add))
                for n in range(3):
                    y, new = rstd[n % 2], rstd[(n + 1) % 2]
                    ch(v.tensor_tensor(nt[:], y[:], y[:], ALU.mult))
                    ch(v.scalar_tensor_tensor(nt[:], nt[:], -0.5, ve[:], ALU.mult, ALU.mult))
                    ch(v.scalar_tensor_tensor(new[:], nt[:], 1.5, y[:], ALU.add, ALU.mult))

            def normalise(a, _, p, ch):
                dve.wait_ge(res_added, a * NJ + NJ)
                for J in range(NJ):
                    v.tensor_scalar(pooled[J], pooled[J], mv[:, J, 0:1], rstd[1][:, J:J + 1], ALU.subtract,
                                    ALU.mult).then_inc(h_ready, 1)

            def h_lo_part(a, c):
                dve.wait_ge(hT_hi_done, a * ND + (c + 1))
                v.tensor_tensor(hT_lo[:, c, :], a_ps[c % 2][:], f32(hT_hi[:, c, :]), ALU.subtract).then_inc(hT_done, 1)

            steps = {"XT": xt_lo_part, "PAR": params, "SCAN": scans, "COLS": columns, "ROWMAX": row_max,
                     "ARGS": exp_args, "E": split_e, "PC": split_pc, "USUM": split_usum, "DSUM": row_scale,
                     "U": split_u, "LN": row_stats, "RSTD": row_rstd, "H": normalise}

            def split_y(b, k):
                dve.wait_ge(silu_done, b * NF + (k + 1))
                if k >= 2 or not (isinstance(b, int) and b == 0):
                    dve.wait_ge(fc2_done, b * NF + (k - 1))
                v.tensor_copy(y_hi[k % 2][:], y_f[k % 2][:]).then_inc(yhi_done, 1)
                dve.wait_ge(yhi_done, b * NF + (k + 1))
                v.tensor_tensor(y_lo[k % 2][:], y_f[k % 2][:], f32(y_hi[k % 2][:]), ALU.subtract).then_inc(split_done, 1)

            def finish(b, p):
                dve.wait_ge(fc2_done, b * NF + NF)
                for r in range(NJ):
                    dve.wait_ge(bias_added, b * NJ + (r + 1))
                    v.tensor_tensor(xt[p][:, r, :], z_ps[r][:], xt[p][:, r, :], ALU.add).then_inc(final_done, 1)

            def w_views(g):
                if g < ND:
                    return q1[:, g, :], s1[:, g, :], w1_hi[:, g, :], w1_lo[:, g, :], gam[:, g:g + 1]
                rows = slice((g - ND) * NG, (g - ND + 1) * NG)
                return tuple(t[:, rows, :].rearrange("p k d -> p (k d)") for t in (q2, s2, w2_hi, w2_lo)) + (0.5,)

            def dequantise(g):
                q, sc, _, _, _ = w_views(g)
                dve.wait_ge(w_in[g], 32)
                v.scalar_tensor_tensor(sc, q, -128.0, sc, ALU.add, ALU.mult).then_inc(wf_ready, 1)

            def w_lo_part(g):
                _, wf, hi, lo, factor = w_views(g)
                dve.wait_ge(whi_ready, g + 1)
                if g < ND:
                    dve.wait_ge(beta_done, g + 1)
                v.scalar_tensor_tensor(lo, wf, factor, f32(hi), ALU.mult, ALU.subtract).then_inc(w_ready, 1)

            def ffn(b, p, with_a, first=False):
                ch = Chain(b + 1)
                split_y(b, 0)
                for h in range(2 * NF - 3):
                    if h % 2 == 0:
                        split_y(b, h // 2 + 1)
                    if first:
                        for name, g in DVE_LATE.get(h, []):
                            (dequantise if name == "D" else w_lo_part)(g)
                    if with_a:
                        for name, n in DVE_PLAN.get(h, []):
                            steps[name](b + 1, n, 1 - p, ch)
                if with_a:
                    assert ch.n == A_STEPS, ch.n
                    for c in range(ND):
                        h_lo_part(b + 1, c)
                finish(b, p)

            ch = Chain(0)
            for name, n in in_order(DVE_PLAN, DVE_UNITS):
                if name == "D":
                    dequantise(n)
                elif name == "L":
                    w_lo_part(n)
                else:
                    steps[name](0, n, 0, ch)
                if (name, n) == ("L", 3):
                    link(v.tensor_reduce(b1x[:], y_ps[0][:, 0:ND * NF].rearrange("p (c k) -> p k c", c=ND), AX_X, ALU.add))
                    v.tensor_tensor(b1[:], b1[:], b1x[:], ALU.add).then_inc(b1_ready, 1)
            for c in range(ND):
                h_lo_part(0, c)
            w_lo_part(4)
            ffn(0, 0, True, True)
            ffn(1, 1, True)
            with dve.Fori(1, B // 2 - 1) as i:
                ffn(i * 2, 0, True)
                ffn(i * 2 + 1, 1, True)
            ffn(B - 2, 0, True)
            ffn(B - 1, 1, False)

        @block.tensor
        def _(pe):
            mm = nc.tensor.matmul

            def transpose_x(a, s, p):
                if s == 0:
                    for J in range(NJ):
                        pe.wait_ge(x_in[p][J], a * 8 + (16 - 8 * p))
                if s:
                    pe.wait_ge(xt_ready, a * NJ + s)
                elif not isinstance(a, int):
                    pe.wait_ge(hT_done, a * ND - 1)
                for J in range(NJ):
                    last = nc.tensor.transpose(a_ps[0][:, J * P:(J + 1) * P], xt[p][:, J, s * P:(s + 1) * P], ident[:])
                last.then_inc(xt_tr, 1)

            def project(a, s, p):
                pe.wait_ge(xt_ready, a * NJ + (s + 1))
                if s == 0 and not isinstance(a, int):
                    pe.wait_ge(hT_done, a * ND)
                o = a_ps[1][:]
                mm(o, wc_hi[:, s, :], part_hi[:], start=(s == 0), stop=False)
                mm(o, wc_hi[:, s, :], part_lo[:], start=False, stop=False)
                mm(o, wc_lo[:, s, :], part_hi[:], start=False, stop=(s == ND - 1)).then_inc(at_done, 1)

            def scores(a, _, p):
                pe.wait_ge(tanh_done, a + 1)
                mm(a_ps[0][:], v_bc[:], th, start=True, stop=True).then_inc(sc_mm, 1)

            def u_sum(a, L, p):
                if L == 0:
                    pe.wait_ge(e_ready, a + 1)
                pe.wait_ge(xs_ready, a * 8 + (L + 1))
                mm(a_ps[0][:], e_cols[:, L, :], xs_hi[:], start=(L == 0), stop=False)
                mm(a_ps[0][:], e_cols[:, L, :], xs_lo[:], start=False, stop=(L == NJ - 1)).then_inc(xs_used, 1)

            def e_sums(a, _, p):
                for L in range(NJ):
                    last = mm(a_ps[1][:, 0:P], e_cols[:, L, :], ones[:], start=(L == 0), stop=(L == NJ - 1))
                last.then_inc(usum_done, 1)

            def p_sums(a, _, p):
                pe.wait_ge(pc_ready, a + 1)
                pe.wait_ge(usum_ready, a + 1)
                mm(a_ps[1][:], ones[:], part_hi[:], start=True, stop=False)
                mm(a_ps[1][:], ones[:], part_lo[:], start=False, stop=False)
                mm(a_ps[1][:], u_sums[:], coef_hi[:], start=False, stop=False)
                last = mm(a_ps[1][:], u_sums[:], coef_lo[:], start=False, stop=True)
                last.then_inc(dsum_done, 1)

            def pool_block(a, J, p):
                o, cols = a_ps[J % 2][:], slice(J * P, (J + 1) * P)
                if J == 0:
                    pe.wait_ge(u_ready, a + 1)
                elif J == 1:
                    pe.wait_ge(c_ready, a + 1)
                else:
                    pe.wait_ge(pooled_done, a * NJ + (J - 1))
                pe.wait_ge(xs_ready, a * 8 + (NJ + J + 1))
                mm(o, part_hi[:, cols], xs_hi[:], start=True, stop=False)
                mm(o, part_hi[:, cols], xs_lo[:], start=False, stop=False)
                mm(o, part_lo[:, cols], xs_hi[:], start=False, stop=False).then_inc(xs_used, 1)
                mm(o, coef_hi[:, cols], u_rows[:], start=False, stop=False)
                mm(o, coef_lo[:, cols], u_rows[:], start=False, stop=True).then_inc(pz_done, 1)

            def transpose_h(a, c):
                if c == 0:
                    pe.wait_ge(h_ready, a * NJ + NJ)
                if c >= 2:
                    pe.wait_ge(hT_done, a * ND + (c - 1))
                for J in range(NJ):
                    last = nc.tensor.transpose(a_ps[c % 2][:, J * P:(J + 1) * P], pooled[J][:, c * P:(c + 1) * P], ident[:])
                last.then_inc(h_tr, 1)

            steps = {"T": transpose_x, "AT": project, "SC": scores, "U": u_sum, "USUM": e_sums, "DSUM": p_sums,
                     "PZ": pool_block}

            def fc1(b, k):
                if k < 2:
                    pe.wait_ge(hT_done, b * ND + ND)
                if k >= 2 or not (isinstance(b, int) and b == 0):
                    pe.wait_ge(silu_done, b * NF + (k - 1))
                o, cols = y_ps[k % 2][:], slice(k * P, (k + 1) * P)
                for c in range(ND):
                    mm(o, w1_hi[:, c, cols], hT_hi[:, c, :], start=(c == 0), stop=False)
                    mm(o, w1_hi[:, c, cols], hT_lo[:, c, :], start=False, stop=False)
                    last = mm(o, w1_lo[:, c, cols], hT_hi[:, c, :], start=False, stop=(c == ND - 1))
                last.then_inc(fc1_done, 1)

            def fc2(b, k):
                if isinstance(b, int) and b == 0 and k % NG == 0:
                    pe.wait_ge(w_ready, ND + k // NG + 1)
                pe.wait_ge(split_done, b * NF + (k + 1))
                if k == 0 and not (isinstance(b, int) and b == 0):
                    pe.wait_ge(final_done, b * NJ)
                for r in range(NJ):
                    rows = slice(r * P, (r + 1) * P)
                    mm(z_ps[r][:], y_hi[k % 2][:, rows], w2_hi[:, k, :], start=(k == 0), stop=False)
                    mm(z_ps[r][:], y_hi[k % 2][:, rows], w2_lo[:, k, :], start=False, stop=False)
                    last = mm(z_ps[r][:], y_lo[k % 2][:, rows], w2_hi[:, k, :], start=False, stop=(k == NF - 1))
                last.then_inc(fc2_done, 1)

            def ffn(b, p, with_a):
                for h in range(LAST):
                    if h % 2 == 0:
                        fc1(b, h // 2 + 2)
                    else:
                        fc2(b, h // 2)
                    if with_a:
                        for name, n in PE_PLAN.get(h, []):
                            steps[name](b + 1, n, 1 - p)
                if with_a:
                    transpose_h(b + 1, 0)
                    transpose_h(b + 1, 1)
                fc2(b, NF - 2)
                if with_a:
                    transpose_h(b + 1, 2)
                    transpose_h(b + 1, 3)
                fc2(b, NF - 1)
                if with_a:
                    fc1(b + 1, 0)
                    fc1(b + 1, 1)

            pe.wait_ge(consts_ready, 1)
            pe.wait_ge(pool_const, POOL_CONSTS)
            def times_beta(c):
                pe.wait_ge(wf_ready, c + 1)
                for k in range(NF):
                    last = mm(y_ps[0][:, c * NF + k:c * NF + k + 1], s1[:, c, k * P:(k + 1) * P], bet[:, c:c + 1],
                              start=True, stop=True)
                last.then_inc(beta_done, 1)

            for name, n in in_order(PE_PLAN, PE_UNITS):
                if name == "B":
                    times_beta(n)
                else:
                    steps[name](0, n, 0)
            for c in range(ND):
                transpose_h(0, c)
            pe.wait_ge(w_ready, ND)
            pe.wait_ge(b1_ready, 1)
            fc1(0, 0)
            fc1(0, 1)
            ffn(0, 0, True)
            ffn(1, 1, True)
            with pe.Fori(1, B // 2 - 1) as i:
                ffn(i * 2, 0, True)
                ffn(i * 2 + 1, 1, True)
            ffn(B - 2, 0, True)
            ffn(B - 1, 1, False)


_INS = ['x', 'itok_B_0_2', 'L0_cond_W1', 'L0_cond_b1', 'L0_cond_v', 'L0_ffn_ln_gamma', 'L0_ffn_ln_beta',
        'L0_ffn_fc1_q', 'L0_ffn_fc1_scales', 'L0_ffn_fc1_bias', 'L0_ffn_fc2_q', 'L0_ffn_fc2_scales',
        'L0_ffn_fc2_bias']


def kernel(**inputs):
    import numpy as _np
    import concourse.bacc as _bacc
    from concourse import mybir as _mybir
    from concourse.bass_utils import run_bass_kernel_spmd as _run

    nc = _bacc.Bacc("TRN2", target_bir_lowering=False, num_devices=1)
    arrays, args = {}, []
    for name in _INS:
        a = _np.ascontiguousarray(inputs[name])
        arrays[f"in_{name}_dram"] = a
        args.append(nc.dram_tensor(f"in_{name}_dram", a.shape, _mybir.dt.from_np(a.dtype), kind="ExternalInput").ap())
    shape = arrays["in_x_dram"].shape
    args.append(nc.dram_tensor("out_0_dram", shape, _mybir.dt.float32, kind="ExternalOutput").ap())
    build(nc, *args)
    r = _run(nc, [arrays], core_ids=[0])
    return r.results[0]["out_0_dram"]
```

```python
from contextlib import ExitStack

import concourse.bass as bass
from concourse import mybir

ALU = mybir.AluOpType
ACT = mybir.ActivationFunctionType
AX_X = mybir.AxisListType.X
F32 = mybir.dt.float32
F32R = mybir.dt.float32r
I32 = mybir.dt.int32

P = 128
Q = 32
NEG = -1e30
EPS = 1e-5


def build(nc, x, itok, cond_w, cond_b, cond_v, gamma, beta, fc1_q, fc1_s, fc1_b, fc2_q, fc2_s, fc2_b, out):
    B, S, D = x.shape
    F = fc1_q.shape[1]
    NJ = S // P
    ND = D // P
    NF = F // P
    NG = NF // ND
    assert tuple(cond_w.shape) == (D, P)
    assert S == 512 and D == 512 and NJ == 4 and ND == 4 and NF == 16 and B % 2 == 0
    SLOT = 514
    POOL_CONSTS = 15
    A_STEPS = 50

    with ExitStack() as ctx:
        def sb(name, shape, dt=F32):
            return ctx.enter_context(nc.sbuf_tensor(name, shape, dt))

        def sem(name):
            return ctx.enter_context(nc.semaphore(name))

        with ExitStack() as raw:
            q1, s1, q2, s2 = (raw.enter_context(nc.sbuf_tensor(name, shape, dt)) for name, shape, dt in (
                ("fc1_codes", [P, ND, F], I32), ("fc1_scaled", [P, ND, F], F32),
                ("fc2_codes", [P, NF, D], I32), ("fc2_scaled", [P, NF, D], F32)))
        w1_hi = sb("w1_hi", [P, ND, F], F32R)
        w1_lo = sb("w1_lo", [P, ND, F], F32R)
        w2_hi = sb("w2_hi", [P, NF, D], F32R)
        w2_lo = sb("w2_lo", [P, NF, D], F32R)
        wc_hi = sb("wc_hi", [P, ND, P], F32R)
        wc_lo = sb("wc_lo", [P, ND, P], F32R)
        hT_hi = sb("hT_hi", [P, ND, S], F32R)
        hT_lo = sb("hT_lo", [P, ND, S], F32R)
        xt = [sb(f"x{p}", [P, NJ, D]) for p in range(2)]
        scratch = sb("scratch", [P, NJ * SLOT])
        xs_hi = [sb(f"xs_hi{i}", [P, D], F32R) for i in range(2)]
        xs_lo = [sb(f"xs_lo{i}", [P, D], F32R) for i in range(2)]
        with ExitStack() as shared:
            h_f = [shared.enter_context(nc.sbuf_tensor(f"h_f{i}", [P, S], F32)) for i in range(2)]
        part_hi = sb("part_hi", [P, S], F32R)
        part_lo = sb("part_lo", [P, S], F32R)
        coef = sb("coef", [P, S], F32R)
        u_rows = sb("u_rows", [P, D], F32R)
        u_sums = sb("u_sums", [P, Q])
        e_all = sb("e_all", [P, NJ, Q])
        y_f = [sb(f"y_f{i}", [P, S]) for i in range(2)]
        y_hi = [sb(f"y_hi{i}", [P, S], F32R) for i in range(2)]
        y_lo = [sb(f"y_lo{i}", [P, S], F32R) for i in range(2)]
        b2h = sb("b2h", [P, D])
        ident = sb("ident", [P, P])
        v_bc = sb("v_bc", [P, P])
        sgn = sb("sgn", [P, P])
        ident_q = sb("ident_q", [P, Q])
        row_kind = sb("row_kind", [P, 4])
        sgn_blk = sb("sgn_blk", [P, NJ])
        pen_sel = sb("pen_sel", [P, NJ])
        pen_own = sb("pen_own", [P, NJ])
        ones = sb("ones", [P, Q])
        b1c = sb("b1c", [P, 1])
        v_col = sb("v_col", [P, 1])
        gam = sb("gam", [P, ND])
        bet = sb("bet", [P, ND])
        b1 = sb("b1", [P, NF])
        tok_i = sb("tok_i", [P, B], I32)
        tok = sb("tok", [P, B])
        is0 = sb("is0", [P, B])
        is1 = sb("is1", [P, B])
        row_i = sb("row_i", [P, NJ], I32)
        blk_i = sb("blk_i", [P, NJ], I32)
        blk_d = sb("blk_d", [P, NJ])
        row_f = sb("row_f", [P, NJ])
        row_a = sb("row_a", [P, NJ])
        row_b = sb("row_b", [P, NJ])
        par = sb("par", [P, B, 8])
        cur = sb("cur", [P, 8])
        pen_p = sb("pen_p", [P, P])
        columns4 = sb("columns4", [P, 12 * NJ])
        taken = iter(range(12))

        def small():
            k = next(taken)
            return columns4[:, k * NJ:(k + 1) * NJ]

        pen_c = small()
        blk_max = small()
        s_col = small()
        e_arg = small()
        m_sel = small()
        m_col = sb("m_col", [P, 1])
        dcnt = small()
        c_row = small()
        stats = sb("stats", [P, NJ, 6])
        mv = sb("mv", [P, NJ, 2])
        ve = small()
        nt = small()
        rs_i = small()
        rstd = [small() for _ in range(2)]

        th = scratch[:, 0:S]
        sc_row = scratch[:, SLOT:SLOT + S]
        fwd = scratch[:, 2 * SLOT:2 * SLOT + S + 1]
        bwd = scratch[:, 3 * SLOT:3 * SLOT + S + 1]
        p_f = scratch[:, 2 * SLOT:2 * SLOT + S]
        c_f = scratch[:, 3 * SLOT:3 * SLOT + S]
        kinds = scratch[:, 0:4 * P].rearrange("p (k n) -> p k n", k=4)
        kinds_d = scratch[:, 2 * SLOT:2 * SLOT + 4 * P].rearrange("p (k n) -> p k n", k=4)
        pooled = [scratch[:, J * SLOT:J * SLOT + D] for J in range(NJ)]
        wc_f = scratch[:, SLOT:SLOT + ND * P]

        def by_block(ap):
            return ap.rearrange("p (j n) -> p j n", j=NJ)

        def f32(ap):
            return ap.bitcast(F32)

        def bank(name):
            return ctx.enter_context(nc.psum_tensor(name, [P, 512], F32))

        z_ps = [bank(f"z_ps{r}") for r in range(NJ)]
        y_ps = [bank(f"y_ps{i}") for i in range(2)]
        a_ps = [bank(f"a_ps{i}") for i in range(2)]

        cond_in = sem("cond_in")
        const_in = sem("const_in")
        tok_in = sem("tok_in")
        bias_in = sem("bias_in")
        x_in = [[sem(f"x_in{p}_{J}") for J in range(NJ)] for p in range(2)]
        stored = [sem(f"stored{J}") for J in range(NJ)]
        pool_const = sem("pool_const")
        dve_const = sem("dve_const")
        dve_step = sem("dve_step")
        cond_ready = sem("cond_ready")
        w_in = [sem(f"w_in{g}") for g in range(2 * ND)]
        codes_f = sem("codes_f")
        w_unit = [sem(f"w_unit{g}") for g in range(2 * ND)]
        xt_tr = sem("xt_tr")
        xt_hi = sem("xt_hi")
        xt_ready = sem("xt_ready")
        at_done = sem("at_done")
        tanh_done = sem("tanh_done")
        sc_mm = sem("sc_mm")
        sc_ready = sem("sc_ready")
        args_ready = sem("args_ready")
        exp_done = sem("exp_done")
        pc_ready = sem("pc_ready")
        xs_ready = sem("xs_ready")
        xs_used = sem("xs_used")
        usum_done = sem("usum_done")
        usum_ready = sem("usum_ready")
        dsum_done = sem("dsum_done")
        c_ready = sem("c_ready")
        u_done = sem("u_done")
        u_hi = sem("u_hi")
        u_ready = sem("u_ready")
        pz_done = sem("pz_done")
        pooled_done = sem("pooled_done")
        res_added = sem("res_added")
        bias_added = sem("bias_added")
        h_ready = sem("h_ready")
        h_tr = sem("h_tr")
        h_affine = sem("h_affine")
        hT_hi_done = sem("hT_hi_done")
        hT_done = sem("hT_done")
        fc1_done = sem("fc1_done")
        silu_done = sem("silu_done")
        yhi_done = sem("yhi_done")
        split_done = sem("split_done")
        fc2_done = sem("fc2_done")
        final_done = sem("final_done")
        last_rows = sem("last_rows")

        LAST = 2 * NF - 4
        PE_PLAN = {3: [("T", 0)], 4: [("AT", 0), ("T", 1)], 5: [("AT", 1), ("T", 2)], 6: [("AT", 2), ("T", 3)],
                   7: [("AT", 3)], 8: [("SC", 0)], 14: [("USUM", 0), ("U", 0)], 16: [("DSUM", 0)],
                   18: [("PZ", 0)], 19: [("PZ", 1)], 20: [("PZ", 2)], 21: [("PZ", 3)]}
        ACT_PLAN = {3: [("XT", 0)], 4: [("XT", 1)], 5: [("XT", 2)], 6: [("XT", 3)], 7: [("TANH", 0)],
                    8: [("SC", 0)], 12: [("EXP", 0)], 14: [("U", 0)], 18: [("PZ", 0)], 19: [("PZ", 1)],
                    20: [("PZ", 2)], 21: [("PZ", 3)]}
        DVE_PLAN = {3: [("XT", 0)], 4: [("XT", 1)], 5: [("XT", 2)], 6: [("XT", 3)], 7: [("PAR", 0)],
                    8: [("SCAN", 0)], 9: [("COLS", 0)], 10: [("ROWMAX", 0)], 11: [("ARGS", 0)], 12: [("XS", 0)],
                    13: [("PC", 0)], 14: [("USUM", 0)], 15: [("U", 0), ("XS", 1)], 16: [("DSUM", 0)],
                    18: [("LN", 0), ("XS", 2)], 19: [("LN", 1), ("XS", 3)], 20: [("LN", 2)], 21: [("LN", 3)],
                    22: [("RSTD", 0)], 23: [("H", 0)]}

        PE_FIRST = [("T", 0), ("T", 1), ("AT", 0), ("T", 2), ("AT", 1), ("T", 3), ("AT", 2), ("AT", 3), ("SC", 0),
                    ("USUM", 0), ("U", 0), ("DSUM", 0),
                    ("PZ", 0), ("PZ", 1), ("PZ", 2), ("PZ", 3)]
        ACT_FIRST = [("XT", 0), ("XT", 1), ("XT", 2), ("XT", 3), ("TANH", 0), ("C", 0), ("SC", 0), ("C", 1), ("H", 0),
                     ("C", 2), ("EXP", 0), ("H", 1), ("U", 0), ("C", 3), ("H", 2), ("PZ", 0), ("PZ", 1),
                     ("PZ", 2), ("PZ", 3), ("H", 3), ("C", 4)]
        DVE_FIRST = [("XT", 0), ("XT", 1), ("KINDS", 0), ("XT", 2), ("XT", 3), ("PAR", 0), ("XS", 0),
                     ("SCAN", 0), ("COLS", 0), ("ROWMAX", 0), ("ARGS", 0), ("XS", 1), ("USUM", 0), ("PC", 0),
                     ("U", 0), ("XS", 2), ("XS", 3), ("DSUM", 0), ("L", 0), ("L", 1), ("LN", 0), ("LN", 1), ("LN", 2), ("LN", 3),
                     ("RSTD", 0), ("H", 0), ("L", 2)]
        POOL_FIRST = [0, 1, 2, 3]
        DVE_LATE = {0: [("D", 5)], 1: [("D", 6)], 2: [("L", 5)], 7: [("L", 6)], 13: [("D", 7)], 20: [("L", 7)]}
        ACT_LATE = {0: [("H", 5)], 2: [("H", 6)], 15: [("H", 7)]}

        def is_first(a):
            return isinstance(a, int) and a == 0

        def is_last(b):
            return isinstance(b, int) and b == B - 1

        def xs_buffers(a, n):
            return (hT_hi[:, n, :], hT_lo[:, n, :]) if is_first(a) else (xs_hi[n % 2][:], xs_lo[n % 2][:])

        def xt_buffers(a, s):
            if is_first(a) and s % 2:
                return y_ps[0], y_hi[0], y_lo[0]
            return a_ps[0], part_hi, part_lo

        def xt_behind(a):
            return 2 if is_first(a) else 1

        def w_views(g):
            if g < ND:
                return q1[:, g, :], s1[:, g, :], w1_hi[:, g, :], w1_lo[:, g, :]
            rows = slice((g - ND) * NG, (g - ND + 1) * NG)
            return tuple(t[:, rows, :].rearrange("p k d -> p (k d)") for t in (q2, s2, w2_hi, w2_lo))

        def w_lo_part(engine, e, g):
            _, wf, hi, lo = w_views(g)
            e.wait_ge(w_unit[g], 2)
            if g < ND:
                engine.tensor_tensor(lo, wf, f32(hi), ALU.subtract).then_inc(w_unit[g], 1)
            else:
                engine.scalar_tensor_tensor(lo, wf, 0.5, f32(hi), ALU.mult, ALU.subtract).then_inc(w_unit[g], 1)

        block = ctx.enter_context(nc.Block())

        @block.sync
        def _(sp):
            x_dram = x.rearrange("b (j p) d -> (b j) p d", p=P)
            out_dram = out.rearrange("b (j p) d -> (b j) p d", p=P)

            def load_x(a, p):
                for J in range(NJ):
                    sp.dma_start(xt[p][:, J, :], x_dram[bass.ds(a * NJ + J, 1), :, :].rearrange("a p d -> p (a d)")).then_inc(x_in[p][J], 16)

            def store(b, p, J):
                sp.wait_ge(final_done, b * NJ + (J + 1))
                sp.dma_start(out_dram[bass.ds(b * NJ + J, 1), :, :].rearrange("a p d -> p (a d)"), xt[p][:, J, :]).then_inc(stored[J], 16)

            sp.dma_start(tok_i[:], itok.rearrange("(o d) -> o d", o=1).to_broadcast([P, B])).then_inc(tok_in, 16)
            sp.dma_start(wc_f.rearrange("p (c a) -> p c a", c=ND), cond_w.rearrange("(c p) a -> p c a", p=P)).then_inc(cond_in, 16)
            load_x(0, 0)
            sp.dma_start(v_col[:], cond_v.rearrange("(p o) -> p o", o=1)).then_inc(cond_in, 16)
            sp.dma_start(b1c[:], cond_b.rearrange("(p o) -> p o", o=1)).then_inc(cond_in, 16)
            sp.dma_start(gam[:], gamma.rearrange("(c p) -> p c", p=P), allow_slow_non_contiguous=True).then_inc(const_in, 16)
            sp.dma_start(bet[:], beta.rearrange("(c p) -> p c", p=P), allow_slow_non_contiguous=True).then_inc(const_in, 16)
            sp.dma_start(b1[:], fc1_b.rearrange("(c p) -> p c", p=P), allow_slow_non_contiguous=True).then_inc(const_in, 16)
            sp.dma_start(b2h[:], fc2_b.rearrange("(o d) -> o d", o=1).to_broadcast([P, D])).then_inc(bias_in, 16)
            for c in range(ND):
                sp.dma_start(q1[:, c, :], fc1_q[c * P:(c + 1) * P, :]).then_inc(w_in[c], 16)
                sp.dma_start(s1[:, c, :], fc1_s[c:c + 1, :].to_broadcast([P, F])).then_inc(w_in[c], 16)
            for g in range(ND):
                rows = slice(g * NG, (g + 1) * NG)
                sp.dma_start(q2[:, rows, :], fc2_q[g * NG * P:(g + 1) * NG * P, :].rearrange("(k p) d -> p k d", p=P)).then_inc(w_in[ND + g], 16)
                sp.dma_start(s2[:, rows, :], fc2_s[rows, :].rearrange("(o k) d -> o k d", o=1).to_broadcast([P, NG, D])).then_inc(w_in[ND + g], 16)
            load_x(1, 1)

            def turn(b, p):
                for J in range(NJ):
                    store(b - 1, p, J)
                for J in range(NJ):
                    sp.wait_ge(stored[J], b * 16)
                    sp.dma_start(xt[p][:, J, :], x_dram[bass.ds((b + 1) * NJ + J, 1), :, :].rearrange("a p d -> p (a d)")).then_inc(x_in[p][J], 16)

            with sp.Fori(0, B // 2 - 1) as i:
                turn(i * 2 + 1, 0)
                turn(i * 2 + 2, 1)
            for b in (B - 2, B - 1):
                for J in range(NJ):
                    store(b, b % 2, J)
            for J in range(NJ):
                sp.wait_ge(stored[J], 16 * B)

        @block.gpsimd
        def _(pool):
            done = [0]

            def link(ins):
                done[0] += 1
                ins.then_inc(pool_const, 1)
                pool.wait_ge(pool_const, done[0])

            link(nc.gpsimd.memset(ident[:], 0.0))
            link(nc.gpsimd.affine_select(out=ident[:], in_=ident[:], compare_op=ALU.not_equal, fill=1.0, base=0,
                                         pattern=[[-1, P]], channel_multiplier=1))
            link(nc.gpsimd.iota(row_i[:], pattern=[[P, NJ]], base=0, channel_multiplier=1))
            link(nc.gpsimd.memset(sgn[:], 0.0))
            link(nc.gpsimd.affine_select(out=sgn[:], in_=sgn[:], compare_op=ALU.is_ge, fill=1.0, base=0,
                                         pattern=[[-1, P]], channel_multiplier=1))
            link(nc.gpsimd.affine_select(out=sgn[:], in_=sgn[:], compare_op=ALU.is_ge, fill=-1.0, base=0,
                                         pattern=[[1, P]], channel_multiplier=-1))
            link(nc.gpsimd.iota(blk_i[:], pattern=[[1, NJ]], base=0, channel_multiplier=0))
            link(nc.gpsimd.memset(kinds, 0.0))
            for L in range(NJ):
                link(nc.gpsimd.memset(kinds[:, 0, L * Q:(L + 1) * Q], float(L)))
            for kind, row, value in ((1, 2, -1.0), (2, 1, -1.0), (3, 0, 1.0)):
                link(nc.gpsimd.memset(kinds[:, kind, :].rearrange("p (q n) -> p q n", n=Q)[:, :, row:row + 1], value))
            assert done[0] == POOL_CONSTS

            def scale_codes(g):
                q, sc, _, _ = w_views(g)
                pool.wait_ge(codes_f, g + 1)
                nc.gpsimd.tensor_tensor(sc, q.bitcast(F32), sc, ALU.mult).then_inc(w_unit[g], 1)

            def residual(a, p, J):
                pool.wait_ge(pooled_done, a * NJ + (J + 1))
                nc.gpsimd.tensor_tensor(xt[p][:, J, :], xt[p][:, J, :], pooled[J], ALU.add).then_inc(res_added, 1)

            def bias(a, p, J):
                pool.wait_ge(res_added, a * NJ + (J + 1))
                nc.gpsimd.tensor_tensor(xt[p][:, J, :], xt[p][:, J, :], b2h[:], ALU.add).then_inc(bias_added, 1)

            def stage_a(a, p):
                for J in range(NJ):
                    residual(a, p, J)
                if is_first(a):
                    w_lo_part(nc.gpsimd, pool, 3)
                    scale_codes(ND)
                for J in range(NJ):
                    bias(a, p, J)

            pool.wait_ge(bias_in, 16)
            link(nc.gpsimd.tensor_scalar(b2h[:], b2h[:], 0.5, None, ALU.mult))
            for g in POOL_FIRST:
                scale_codes(g)
            stage_a(0, 0)
            with pool.Fori(0, B // 2 - 1) as i:
                stage_a(i * 2 + 1, 1)
                stage_a(i * 2 + 2, 0)
            stage_a(B - 1, 1)

        @block.scalar
        def _(act):
            def copy(o, i):
                return nc.scalar.activation(o, i, ACT.Copy)

            def xt_hi_part(a, s):
                act.wait_ge(xt_tr, a * NJ + (s + 1))
                if s >= xt_behind(a):
                    act.wait_ge(at_done, a * NJ + (s + 1 - xt_behind(a)))
                bank, hi, _ = xt_buffers(a, s)
                copy(hi[:], bank[:]).then_inc(xt_hi, 1)

            def tanh(a, _):
                if is_first(a):
                    act.wait_ge(cond_in, 16 * 3)
                act.wait_ge(at_done, a * NJ + NJ)
                nc.scalar.activation(th, a_ps[1][:], ACT.Tanh, bias=b1c[:, 0:1]).then_inc(tanh_done, 1)

            def scores(a, _):
                act.wait_ge(sc_mm, a + 1)
                copy(sc_row, a_ps[0][:]).then_inc(sc_ready, 1)

            def exps(a, _):
                act.wait_ge(args_ready, a + 1)
                nc.scalar.activation(e_all[:, :, 0:3], e_arg[:].rearrange("p (j o) -> p j o", o=1).to_broadcast([P, NJ, 3]),
                                     ACT.Exp).then_inc(exp_done, 1)
                nc.scalar.activation(c_f, c_f, ACT.Exp, bias=m_col[:, 0:1]).then_inc(exp_done, 1)
                for J in range(NJ):
                    blk = p_f[:, J * P:(J + 1) * P]
                    nc.scalar.activation(blk, blk, ACT.Exp, bias=s_col[:, J:J + 1]).then_inc(exp_done, 1)

            def u_hi_part(a, _):
                act.wait_ge(u_done, a + 1)
                copy(u_rows[:], a_ps[0][:]).then_inc(u_hi, 1)

            def pool_rows(a, J):
                if J == 0:
                    act.wait_ge(c_ready, a + 1)
                act.wait_ge(pz_done, a * NJ + (J + 1))
                nc.scalar.activation(pooled[J], a_ps[J % 2][:], ACT.Copy, scale=c_row[:, J:J + 1]).then_inc(pooled_done, 1)

            def h_scaled(a, c):
                act.wait_ge(h_tr, a * ND + (c + 1))
                if c >= 2:
                    act.wait_ge(hT_done, a * ND + (c - 1))
                nc.scalar.activation(h_f[c % 2][:], a_ps[c % 2][:], ACT.Identity, bias=bet[:, c:c + 1],
                                     scale=gam[:, c:c + 1]).then_inc(h_affine, 1)

            steps = {"XT": xt_hi_part, "TANH": tanh, "SC": scores, "EXP": exps, "U": u_hi_part, "PZ": pool_rows}

            def silu(b, k):
                act.wait_ge(fc1_done, b * NF + (k + 1))
                if k >= 2 or not is_first(b):
                    act.wait_ge(split_done, b * NF + (k - 1))
                nc.scalar.activation(y_f[k % 2][:], y_ps[k % 2][:], ACT.Silu, bias=b1[:, k:k + 1]).then_inc(silu_done, 1)

            def float_codes(g):
                q = w_views(g)[0]
                act.wait_ge(w_in[g], 32)
                nc.scalar.activation(q.bitcast(F32), q, ACT.Copy, bias=-128.0).then_inc(codes_f, 1)

            def w_hi_part(g):
                _, wf, hi, _ = w_views(g)
                act.wait_ge(w_unit[g], 1)
                nc.scalar.activation(hi, wf, ACT.Copy, scale=1.0 if g < ND else 0.5).then_inc(w_unit[g], 1)

            def ffn(b, with_a, first=False):
                for k in range(2):
                    silu(b, k)
                    if first and k == 0:
                        w_hi_part(ND)
                for h in range(LAST):
                    if h % 2 == 0:
                        silu(b, h // 2 + 2)
                    if first:
                        for _, g in ACT_LATE.get(h, []):
                            w_hi_part(g)
                    if with_a:
                        for name, n in ACT_PLAN.get(h, []):
                            steps[name](b + 1, n)
                if with_a:
                    for c in range(ND):
                        h_scaled(b + 1, c)

            for name, n in ACT_FIRST:
                if name == "H":
                    w_hi_part(n)
                elif name == "C":
                    float_codes(n)
                else:
                    steps[name](0, n)
            act.wait_ge(const_in, 16 * 3)
            for c in range(ND):
                h_scaled(0, c)
            ffn(0, True, True)
            ffn(1, True)
            with act.Fori(1, B // 2 - 1) as i:
                ffn(i * 2, True)
                ffn(i * 2 + 1, True)
            ffn(B - 2, True)
            ffn(B - 1, False)

        @block.vector
        def _(dve):
            v = nc.vector
            done = [0]

            def link(ins):
                done[0] += 1
                ins.then_inc(dve_const, 1)
                dve.wait_ge(dve_const, done[0])

            link(v.memset(e_all[:], 0.0))
            link(v.memset(ones[:], 1.0))
            dve.wait_ge(tok_in, 16)
            link(v.tensor_copy(tok[:], tok_i[:]))
            link(v.tensor_scalar(is0[:], tok[:], 0.0, None, ALU.is_equal))
            link(v.tensor_scalar(is1[:], tok[:], 1.0, None, ALU.is_equal))
            link(v.tensor_tensor(par[:, :, 0], is1[:], is0[:], ALU.subtract))
            link(v.tensor_scalar(par[:, :, 1], tok[:], 0.0, NEG, ALU.not_equal, ALU.mult))
            link(v.tensor_scalar(par[:, :, 2], tok[:], 1.0, NEG, ALU.not_equal, ALU.mult))
            link(v.tensor_scalar(par[:, :, 3], par[:, :, 0], 0.0, NEG, ALU.not_equal, ALU.mult))
            dve.wait_ge(pool_const, 3)
            link(v.tensor_copy(row_f[:], row_i[:]))
            link(v.tensor_scalar(row_a[:], row_f[:], float(S - 2), None, ALU.subtract))
            link(v.tensor_scalar(row_b[:], row_f[:], -1.0, 1.0, ALU.mult, ALU.add))
            for J in range(NJ):
                cnt = par[:, :, 4 + J]
                link(v.tensor_scalar(cnt, is0[:], row_a[:, J:J + 1], float(S - 1), ALU.mult, ALU.add))
                link(v.scalar_tensor_tensor(cnt, is1[:], row_b[:, J:J + 1], cnt, ALU.mult, ALU.add))
            dve.wait_ge(cond_in, 16 * 3)
            link(v.tensor_copy(v_bc[:], v_col[:, 0:1].to_broadcast([P, P])))
            wc_flat = [t[:].rearrange("p c a -> p (c a)") for t in (wc_hi, wc_lo)]
            link(v.tensor_copy(wc_flat[0], wc_f))
            v.tensor_tensor(wc_flat[1], wc_f, f32(wc_flat[0]), ALU.subtract).then_inc(cond_ready, 1)

            def partition_kinds():
                dve.wait_ge(pool_const, POOL_CONSTS)
                link(v.tensor_tensor(kinds_d, kinds, ident[:].rearrange("p (o n) -> p o n", o=1).to_broadcast([P, 4, P]), ALU.mult))
                link(v.tensor_reduce(row_kind[:], kinds_d, AX_X, ALU.add))
                link(v.tensor_reduce(ident_q[:], ident[:].rearrange("p (q n) -> p n q", n=Q), AX_X, ALU.add))
                link(v.tensor_copy(blk_d[:], blk_i[:]))
                link(v.tensor_scalar(blk_d[:], blk_d[:], row_kind[:, 0:1], None, ALU.subtract))
                link(v.tensor_scalar(sgn_blk[:], blk_d[:], 1.0, -1.0, ALU.min, ALU.max))
                link(v.tensor_scalar(pen_sel[:], blk_d[:], 0.0, NEG, ALU.not_equal, ALU.mult))
                link(v.tensor_scalar(pen_own[:], blk_d[:], 0.0, NEG, ALU.is_equal, ALU.mult))

            class Chain:
                def __init__(self, a):
                    self.base, self.n = a * A_STEPS, 0

                def count(self, ins):
                    self.n += 1
                    ins.then_inc(dve_step, 1)

                def wait(self):
                    dve.wait_ge(dve_step, self.base + self.n)

                def __call__(self, ins):
                    self.count(ins)
                    self.wait()

            def xt_lo_part(a, s, p, ch):
                dve.wait_ge(xt_hi, a * NJ + (s + 1))
                bank, hi, lo = xt_buffers(a, s)
                v.tensor_tensor(lo[:], bank[:], f32(hi[:]), ALU.subtract).then_inc(xt_ready, 1)

            def split_x(a, n, p, ch):
                dve.wait_ge(x_in[p][n], a * 8 + (16 - 8 * p))
                if not is_first(a):
                    dve.wait_ge(xs_used, a * NJ + (n - 1))
                hi, lo = xs_buffers(a, n)
                ch(v.tensor_copy(hi, xt[p][:, n, :]))
                v.tensor_tensor(lo, xt[p][:, n, :], f32(hi), ALU.subtract).then_inc(xs_ready, 1)

            def params(a, _, p, ch):
                flat = par[:].rearrange("p b k -> p (b k)")
                ch(v.tensor_copy(cur[:], flat[:, bass.ds(a * 8, 8)]))
                ch(v.tensor_scalar(pen_p[:], sgn[:], cur[:, 0:1], NEG, ALU.is_equal, ALU.mult))
                ch(v.tensor_scalar(pen_c[:], sgn_blk[:], cur[:, 0:1], NEG, ALU.is_equal, ALU.mult))
                ch(v.tensor_tensor(pen_c[:], pen_c[:], pen_own[:], ALU.min))

            def scans(a, _, p, ch):
                dve.wait_ge(sc_ready, a + 1)
                ch(v.memset(fwd[:, 0:1], NEG))
                ch(v.memset(bwd[:, S:S + 1], NEG))
                ch(v.tensor_tensor_scan(fwd[:, 1:S + 1], sc_row, sc_row, NEG, ALU.max, ALU.max))
                ch(v.tensor_tensor_scan(bwd[:, 0:S][:, ::-1], sc_row[:, ::-1], sc_row[:, ::-1], NEG, ALU.max, ALU.max))

            def columns(a, _, p, ch):
                ch(v.tensor_reduce(blk_max[:], by_block(sc_row), AX_X, ALU.max))
                ch(v.tensor_tensor(by_block(th), by_block(sc_row), ident[:].rearrange("p (o n) -> p o n", o=1).to_broadcast([P, NJ, P]), ALU.mult))
                ch(v.tensor_reduce(s_col[:], by_block(th), AX_X, ALU.add))
                ch(v.tensor_tensor(e_arg[:], s_col[:], blk_max[:], ALU.subtract))
                ch(v.tensor_tensor(m_sel[:], blk_max[:], pen_sel[:], ALU.add))
                ch(v.tensor_reduce(m_col[:], m_sel[:], AX_X, ALU.max))

            def row_max(a, _, p, ch):
                ch(v.tensor_tensor(th, fwd[:, 0:S], bwd[:, 1:S + 1], ALU.max))
                ch(v.tensor_scalar(sc_row, fwd[:, 1:S + 1], cur[:, 1:2], None, ALU.add))
                ch(v.scalar_tensor_tensor(sc_row, bwd[:, 0:S], cur[:, 2:3], sc_row, ALU.add, ALU.max))
                ch(v.scalar_tensor_tensor(sc_row, th, cur[:, 3:4], sc_row, ALU.add, ALU.max))

            def exp_args(a, _, p, ch):
                ch(v.tensor_tensor(by_block(p_f), pen_p[:].rearrange("p (o n) -> p o n", o=1).to_broadcast([P, NJ, P]), by_block(sc_row), ALU.subtract))
                v.tensor_tensor(by_block(c_f), pen_c[:].rearrange("p (n o) -> p n o", o=1).to_broadcast([P, NJ, P]), by_block(sc_row),
                                ALU.subtract).then_inc(args_ready, 1)

            def split_pc(a, _, p, ch):
                dve.wait_ge(exp_done, a * 6 + 6)
                ch(v.tensor_copy(part_hi[:], p_f))
                ch(v.tensor_tensor(part_lo[:], p_f, f32(part_hi[:]), ALU.subtract))
                ch(v.tensor_copy(coef[:], c_f))
                v.scalar_tensor_tensor(coef[:], f32(coef[:]), row_kind[:, 1:2], c_f, ALU.mult, ALU.add).then_inc(pc_ready, 1)

            def move_usum(a, _, p, ch):
                dve.wait_ge(usum_done, a + 1)
                v.tensor_scalar(u_sums[:], a_ps[1][:, 0:1].to_broadcast([P, Q]), row_kind[:, 3:4], None, ALU.mult).then_inc(usum_ready, 1)

            def row_scale(a, _, p, ch):
                dve.wait_ge(dsum_done, a + 1)
                ch(v.tensor_tensor(by_block(th[:, 0:P]), by_block(a_ps[1][:, 0:P]),
                                   ident_q[:].rearrange("p (o n) -> p o n", o=1).to_broadcast([P, NJ, Q]), ALU.mult))
                ch(v.tensor_reduce(dcnt[:], by_block(th[:, 0:P]), AX_X, ALU.add))
                ch(v.tensor_tensor(dcnt[:], dcnt[:], cur[:, 4:4 + NJ], ALU.mult))
                v.reciprocal(c_row[:], dcnt[:]).then_inc(c_ready, 1)

            def split_u(a, _, p, ch):
                dve.wait_ge(u_hi, a + 1)
                v.scalar_tensor_tensor(u_rows[:], f32(u_rows[:]), row_kind[:, 2:3], a_ps[0][:], ALU.mult, ALU.add).then_inc(u_ready, 1)

            def row_stats(a, J, p, ch):
                dve.wait_ge(pooled_done, a * NJ + (J + 1))
                ch(v.bn_stats(stats[:, J, :], pooled[J]))

            def row_rstd(a, _, p, ch):
                ch.count(v.memset(ve[:], EPS))
                for J in range(NJ):
                    ch.count(v.bn_aggr(mv[:, J, :], stats[:, J, :]))
                ch.wait()
                ch(v.tensor_tensor(ve[:], mv[:, :, 1], ve[:], ALU.add))
                ch(v.tensor_scalar(rs_i[:].bitcast(I32), ve[:].bitcast(I32), 1, None, ALU.logical_shift_right))
                ch(v.tensor_scalar(rstd[0][:].bitcast(I32), rs_i[:].bitcast(I32), -1.0, float(0x5f3759df), ALU.mult, ALU.add))
                for n in range(3):
                    y, new = rstd[n % 2], rstd[(n + 1) % 2]
                    ch(v.tensor_tensor(nt[:], y[:], y[:], ALU.mult))
                    ch(v.scalar_tensor_tensor(nt[:], nt[:], -0.5, ve[:], ALU.mult, ALU.mult))
                    ch(v.scalar_tensor_tensor(new[:], nt[:], 1.5, y[:], ALU.add, ALU.mult))

            def normalise(a, _, p, ch):
                for J in range(NJ):
                    dve.wait_ge(res_added, a * NJ + (J + 1))
                    v.tensor_scalar(pooled[J], pooled[J], mv[:, J, 0:1], rstd[1][:, J:J + 1], ALU.subtract,
                                    ALU.mult).then_inc(h_ready, 1)

            def split_h(a, c):
                dve.wait_ge(h_affine, a * ND + (c + 1))
                if c == 0 and not is_first(a):
                    dve.wait_ge(fc1_done, a * NF)
                f = h_f[c % 2][:]
                v.tensor_copy(hT_hi[:, c, :], f).then_inc(hT_hi_done, 1)
                dve.wait_ge(hT_hi_done, a * ND + (c + 1))
                v.tensor_tensor(hT_lo[:, c, :], f, f32(hT_hi[:, c, :]), ALU.subtract).then_inc(hT_done, 1)

            steps = {"XT": xt_lo_part, "PAR": params, "SCAN": scans, "COLS": columns, "ROWMAX": row_max,
                     "ARGS": exp_args, "PC": split_pc, "USUM": move_usum, "DSUM": row_scale,
                     "XS": split_x, "U": split_u, "LN": row_stats, "RSTD": row_rstd, "H": normalise}

            def dequantise(g):
                q, sc, _, _ = w_views(g)
                dve.wait_ge(w_in[g], 32)
                v.scalar_tensor_tensor(sc, q, -128.0, sc, ALU.add, ALU.mult).then_inc(w_unit[g], 1)

            def split_y(b, k):
                dve.wait_ge(silu_done, b * NF + (k + 1))
                if k >= 2 or not is_first(b):
                    dve.wait_ge(fc2_done, b * NF + (k - 1))
                v.tensor_copy(y_hi[k % 2][:], y_f[k % 2][:]).then_inc(yhi_done, 1)
                dve.wait_ge(yhi_done, b * NF + (k + 1))
                v.tensor_tensor(y_lo[k % 2][:], y_f[k % 2][:], f32(y_hi[k % 2][:]), ALU.subtract).then_inc(split_done, 1)

            def finish(b, p):
                if not is_last(b):
                    dve.wait_ge(fc2_done, b * NF + NF)
                for r in range(NJ):
                    if is_last(b):
                        dve.wait_ge(last_rows, r + 1)
                    dve.wait_ge(bias_added, b * NJ + (r + 1))
                    v.tensor_tensor(xt[p][:, r, :], z_ps[r][:], xt[p][:, r, :], ALU.add).then_inc(final_done, 1)

            def ffn(b, p, with_a, first=False):
                ch = Chain(b + 1)
                split_y(b, 0)
                if first:
                    w_lo_part(v, dve, ND)
                for h in range(LAST + 1):
                    if h % 2 == 0:
                        split_y(b, h // 2 + 1)
                    if first:
                        for name, g in DVE_LATE.get(h, []):
                            if name == "D":
                                dequantise(g)
                            else:
                                w_lo_part(v, dve, g)
                    if with_a:
                        for name, n in DVE_PLAN.get(h, []):
                            steps[name](b + 1, n, 1 - p, ch)
                if with_a:
                    assert ch.n == A_STEPS, ch.n
                    for c in range(ND):
                        split_h(b + 1, c)
                finish(b, p)

            ch = Chain(0)
            for name, n in DVE_FIRST:
                if name == "L":
                    w_lo_part(v, dve, n)
                elif name == "KINDS":
                    partition_kinds()
                else:
                    steps[name](0, n, 0, ch)
            for c in range(ND):
                split_h(0, c)
            ffn(0, 0, True, True)
            ffn(1, 1, True)
            with dve.Fori(1, B // 2 - 1) as i:
                ffn(i * 2, 0, True)
                ffn(i * 2 + 1, 1, True)
            ffn(B - 2, 0, True)
            ffn(B - 1, 1, False)

        @block.tensor
        def _(pe):
            mm = nc.tensor.matmul

            def transpose_x(a, s, p):
                if s == 0:
                    for J in range(NJ):
                        pe.wait_ge(x_in[p][J], a * 8 + (16 - 8 * p))
                if s >= xt_behind(a):
                    pe.wait_ge(xt_ready, a * NJ + (s + 1 - xt_behind(a)))
                bank = xt_buffers(a, s)[0]
                for J in range(NJ):
                    last = nc.tensor.transpose(bank[:, J * P:(J + 1) * P], xt[p][:, J, s * P:(s + 1) * P], ident[:])
                last.then_inc(xt_tr, 1)

            def project(a, s, p):
                pe.wait_ge(xt_ready, a * NJ + (s + 1))
                if s == 0 and is_first(a):
                    pe.wait_ge(cond_ready, 1)
                o = a_ps[1][:]
                _, hi, lo = xt_buffers(a, s)
                mm(o, wc_hi[:, s, :], hi[:], start=(s == 0), stop=False)
                mm(o, wc_hi[:, s, :], lo[:], start=False, stop=False)
                mm(o, wc_lo[:, s, :], hi[:], start=False, stop=(s == ND - 1)).then_inc(at_done, 1)

            def scores(a, _, p):
                pe.wait_ge(tanh_done, a + 1)
                mm(a_ps[0][:], v_bc[:], th, start=True, stop=True).then_inc(sc_mm, 1)

            def quadrant(q):
                return slice(q * Q, (q + 1) * Q), dict(tile_position=(0, q * Q))

            def u_sum(a, _, p):
                pe.wait_ge(exp_done, a * 6 + 1)
                for L in range(NJ):
                    rows, place = quadrant(L)
                    last = mm(a_ps[0][rows, :], e_all[:, L, :], xt[p][:, L, :], start=True, stop=True, **place)
                last.then_inc(u_done, 1)

            def e_sums(a, _, p):
                pe.wait_ge(exp_done, a * 6 + 1)
                for L in range(NJ):
                    rows, place = quadrant(L)
                    last = mm(a_ps[1][rows, 0:2], e_all[:, L, :], ones[:, 0:2], start=True, stop=True, **place)
                last.then_inc(usum_done, 1)

            def p_sums(a, _, p):
                pe.wait_ge(exp_done, a * 6 + 6)
                pe.wait_ge(usum_ready, a + 1)
                for n, (left, right) in enumerate(((ones, p_f), (u_sums, c_f))):
                    for q in range(P // Q):
                        rows, place = quadrant(q)
                        last = mm(by_block(a_ps[1][rows, 0:P]), left[:], by_block(right)[:, :, rows],
                                  start=(n == 0), stop=(n == 1), **place)
                last.then_inc(dsum_done, 1)

            def pool_block(a, J, p):
                o, cols = a_ps[J % 2][:], slice(J * P, (J + 1) * P)
                if J == 0:
                    pe.wait_ge(pc_ready, a + 1)
                    pe.wait_ge(u_ready, a + 1)
                elif J == 1:
                    pe.wait_ge(c_ready, a + 1)
                else:
                    pe.wait_ge(pooled_done, a * NJ + (J - 1))
                pe.wait_ge(xs_ready, a * NJ + (J + 1))
                hi, lo = xs_buffers(a, J)
                mm(o, part_hi[:, cols], hi, start=True, stop=False)
                mm(o, part_hi[:, cols], lo, start=False, stop=False)
                mm(o, part_lo[:, cols], hi, start=False, stop=False).then_inc(xs_used, 1)
                mm(o, coef[:, cols], u_rows[:], start=False, stop=True).then_inc(pz_done, 1)

            def transpose_h(a, c):
                if c == 0:
                    pe.wait_ge(h_ready, a * NJ + NJ)
                if c >= 2:
                    pe.wait_ge(h_affine, a * ND + (c - 1))
                for J in range(NJ):
                    last = nc.tensor.transpose(a_ps[c % 2][:, J * P:(J + 1) * P], pooled[J][:, c * P:(c + 1) * P], ident[:])
                last.then_inc(h_tr, 1)

            steps = {"T": transpose_x, "AT": project, "SC": scores, "U": u_sum, "USUM": e_sums, "DSUM": p_sums,
                     "PZ": pool_block}

            def fc1(b, k):
                if k >= 2 or not is_first(b):
                    pe.wait_ge(silu_done, b * NF + (k - 1))
                o, cols = y_ps[k % 2][:], slice(k * P, (k + 1) * P)
                for c in range(ND):
                    if k == 0:
                        pe.wait_ge(hT_done, b * ND + (c + 1))
                        if is_first(b):
                            pe.wait_ge(w_unit[c], 3)
                    mm(o, w1_hi[:, c, cols], hT_hi[:, c, :], start=(c == 0), stop=False)
                    mm(o, w1_hi[:, c, cols], hT_lo[:, c, :], start=False, stop=False)
                    last = mm(o, w1_lo[:, c, cols], hT_hi[:, c, :], start=False, stop=(c == ND - 1))
                last.then_inc(fc1_done, 1)

            def fc2(b, k):
                if is_first(b) and k % NG == 0:
                    pe.wait_ge(w_unit[ND + k // NG], 3)
                pe.wait_ge(split_done, b * NF + (k + 1))
                if k == 0 and not is_first(b):
                    pe.wait_ge(final_done, b * NJ)
                for r in range(NJ):
                    rows = slice(r * P, (r + 1) * P)
                    mm(z_ps[r][:], y_hi[k % 2][:, rows], w2_hi[:, k, :], start=(k == 0), stop=False)
                    mm(z_ps[r][:], y_hi[k % 2][:, rows], w2_lo[:, k, :], start=False, stop=False)
                    last = mm(z_ps[r][:], y_lo[k % 2][:, rows], w2_hi[:, k, :], start=False, stop=(k == NF - 1))
                    if is_last(b) and k == NF - 1:
                        last.then_inc(last_rows, 1)
                if not (is_last(b) and k == NF - 1):
                    last.then_inc(fc2_done, 1)

            def ffn(b, p, with_a):
                for h in range(LAST):
                    if h % 2 == 0:
                        fc1(b, h // 2 + 2)
                    else:
                        fc2(b, h // 2)
                    if with_a:
                        for name, n in PE_PLAN.get(h, []):
                            steps[name](b + 1, n, 1 - p)
                if with_a:
                    transpose_h(b + 1, 0)
                    transpose_h(b + 1, 1)
                fc2(b, NF - 2)
                if with_a:
                    transpose_h(b + 1, 2)
                    transpose_h(b + 1, 3)
                fc2(b, NF - 1)
                if with_a:
                    fc1(b + 1, 0)
                    fc1(b + 1, 1)

            pe.wait_ge(pool_const, 2)
            for name, n in PE_FIRST:
                steps[name](0, n, 0)
            for c in range(ND):
                transpose_h(0, c)
            fc1(0, 0)
            fc1(0, 1)
            ffn(0, 0, True)
            ffn(1, 1, True)
            with pe.Fori(1, B // 2 - 1) as i:
                ffn(i * 2, 0, True)
                ffn(i * 2 + 1, 1, True)
            ffn(B - 2, 0, True)
            ffn(B - 1, 1, False)


_INS = ['x', 'itok_B_0_2', 'L0_cond_W1', 'L0_cond_b1', 'L0_cond_v', 'L0_ffn_ln_gamma', 'L0_ffn_ln_beta',
        'L0_ffn_fc1_q', 'L0_ffn_fc1_scales', 'L0_ffn_fc1_bias', 'L0_ffn_fc2_q', 'L0_ffn_fc2_scales',
        'L0_ffn_fc2_bias']


def kernel(**inputs):
    import numpy as _np
    import concourse.bacc as _bacc
    from concourse import mybir as _mybir
    from concourse.bass_utils import run_bass_kernel_spmd as _run

    nc = _bacc.Bacc("TRN2", target_bir_lowering=False, num_devices=1)
    arrays, args = {}, []
    for name in _INS:
        a = _np.ascontiguousarray(inputs[name])
        arrays[f"in_{name}_dram"] = a
        args.append(nc.dram_tensor(f"in_{name}_dram", a.shape, _mybir.dt.from_np(a.dtype), kind="ExternalInput").ap())
    shape = arrays["in_x_dram"].shape
    args.append(nc.dram_tensor("out_0_dram", shape, _mybir.dt.float32, kind="ExternalOutput").ap())
    build(nc, *args)
    r = _run(nc, [arrays], core_ids=[0])
    return r.results[0]["out_0_dram"]
```
